# Optimizing a Trainium2 kernel written in Bass

```python
import numpy as np
import jax
import jax.numpy as jnp

def _softmax(x, axis=-1):
    return jax.nn.softmax(x, axis=axis)

def _gelu(x):
    return jax.nn.gelu(x, approximate=True)

def _silu(x):
    return jax.nn.silu(x)

def _sigmoid(x):
    return jax.nn.sigmoid(x)

def _layernorm(x, axis=-1, eps=1e-05):
    m = jnp.mean(x, axis=axis, keepdims=True)
    v = jnp.var(x, axis=axis, keepdims=True)
    return (x - m) / jnp.sqrt(v + eps)

def _scatter_add(tgt, idx, src, axis=0):
    return tgt.at[idx].add(src)

def _segment_sum(src, seg, n):
    return jax.ops.segment_sum(src, seg, n)
kernel_name = 'mk_gnn_resnorm_d1_gnn_r64_1eed80'

def setup_inputs(seed: int=0):
    np.random.seed(seed)
    _w = jnp.asarray

    def _rec_inputs():
        import jax
        import jax.numpy as jnp
        _gk = jax.random.key(seed)
        x = -0.0006008 + 1.001 * jax.random.normal(jax.random.fold_in(_gk, 1), (100000, 128), jnp.float32)
        src = jax.random.randint(jax.random.fold_in(_gk, 2), (50000,), 0, 100000, jnp.int32)
        dst = jax.random.randint(jax.random.fold_in(_gk, 3), (50000,), 0, 100000, jnp.int32)
        _o = jnp.argsort(dst, stable=True)
        src = src[_o]
        dst = dst[_o]
        edge_attr_64 = -0.000128692 + 0.999872 * jax.random.normal(jax.random.fold_in(_gk, 12), (50000, 64), jnp.float32)
        return (x, src, dst, edge_attr_64)
    x, src, dst, edge_attr_64 = _rec_inputs()

    def _L0_gnn_setup():
        import jax, jax.numpy as jnp
        import numpy as np
        N_NODES = 20000
        N_EDGES = 10000
        D_NODE = 128
        D_EDGE = 64
        D_OUT = 128
        key = jax.random.key(seed)
        ks = jax.random.split(key, 7)
        feats_node = jax.random.normal(ks[0], (N_NODES, D_NODE), dtype=jnp.float32)
        feats_edge = jax.random.normal(ks[1], (N_EDGES, D_EDGE), dtype=jnp.float32)
        Wn = 0.5 * jax.random.normal(ks[2], (D_OUT, D_NODE), dtype=jnp.float32)
        We = 0.5 * jax.random.normal(ks[3], (D_OUT, D_EDGE), dtype=jnp.float32)
        Wa = 0.5 * jax.random.normal(ks[4], (1, 3 * D_OUT), dtype=jnp.float32)
        src = jax.random.randint(ks[5], (N_EDGES,), 0, N_NODES, dtype=jnp.int32)
        dst = jax.random.randint(ks[6], (N_EDGES,), 0, N_NODES, dtype=jnp.int32)
        return {'feats_node': feats_node, 'feats_edge': feats_edge, 'Wn': Wn, 'We': We, 'Wa': Wa, 'src': src, 'dst': dst}
    _L0_gnn_all = _L0_gnn_setup()
    _L0_gnn_in = {k: v for k, v in _L0_gnn_all.items() if k in ('Wn', 'We', 'Wa')}
    del _L0_gnn_all
    return {'x': x, 'src': src, 'dst': dst, 'edge_attr_64': edge_attr_64, 'L0_gnn_Wn': _L0_gnn_in['Wn'], 'L0_gnn_We': _L0_gnn_in['We'], 'L0_gnn_Wa': _L0_gnn_in['Wa']}

def reference(x, src, dst, edge_attr_64, L0_gnn_Wn, L0_gnn_We, L0_gnn_Wa):
    import jax
    import jax.numpy as jnp

    def _L0_gnn_ref(feats_node, feats_edge, Wn, We, Wa, src, dst):
        import jax, jax.numpy as jnp
        import numpy as np
        N_NODES = 20000
        N_EDGES = 10000
        D_NODE = 128
        D_EDGE = 64
        D_OUT = 128
        n_nodes = feats_node.shape[0]
        d = Wn.shape[0]
        z_node = feats_node @ Wn.T
        z_edge = feats_edge @ We.T
        a_src, a_dst, a_e = (Wa[0, :d], Wa[0, d:2 * d], Wa[0, 2 * d:])
        z_src = z_node[src]
        z_dst = z_node[dst]
        logits = z_src @ a_src + z_dst @ a_dst + z_edge @ a_e
        e = jax.nn.leaky_relu(logits, negative_slope=0.2)
        m = jax.ops.segment_max(e, dst, num_segments=n_nodes)
        ex = jnp.exp(e - m[dst])
        s = jax.ops.segment_sum(ex, dst, num_segments=n_nodes)
        alpha = ex / jnp.where(s[dst] == 0, 1.0, s[dst])
        h = jax.ops.segment_sum(alpha[:, None] * z_src, dst, num_segments=n_nodes)
        return h
    x = _layernorm(x + _L0_gnn_ref(x, edge_attr_64, L0_gnn_Wn, L0_gnn_We, L0_gnn_Wa, src, dst), axis=-1)
    return x

_drawn_inputs = setup_inputs


def setup_inputs(seed=0):
    import zlib

    import numpy as np

    out = dict(_drawn_inputs(seed))
    spreads = {}
    factors = {}
    for name, (base, spread) in spreads.items():
        noise = np.random.default_rng([zlib.crc32(name.encode()), seed]).standard_normal(out[name].shape)
        drawn = base * np.exp(spread * noise) if base else spread * noise
        out[name] = jnp.asarray(drawn.astype(out[name].dtype))
    for name, factor in factors.items():
        out[name] = (out[name] * factor).astype(out[name].dtype)
    return out
```

```python
import numpy as np
import concourse.bass as bass
from concourse import mybir
from contextlib import ExitStack

fp32 = mybir.dt.float32
i32 = mybir.dt.int32
ALU = mybir.AluOpType
ACT = mybir.ActivationFunctionType
AX = mybir.AxisListType

P = 128
STEP = 16
RUN = 200
K = 32
Q = 4
QG = K // Q
XL = 8
RING = 4
BIG = 1e38
EPS = 1e-5
SLOPE = 0.2
GUESS = 1597463007.0
NEWTON = 3


def gnn_layer(nc, x, src, dst, edge, Wn, We, Wa, out):
    N, D = x.shape
    E, DE = edge.shape
    NT = -(-N // P)
    LAST = N - (NT - 1) * P
    NB = -(-NT // P)
    GF = NT // K
    TT = NT - GF * K
    TQ = -(-TT // Q)
    LOOPS = (GF - 3) // RING
    WR = (E - P) // STEP + 1
    WR16 = WR // 16 * 16
    NR = E // RUN
    assert E % RUN == 0 and E % STEP == 0 and (E - P) % STEP == 0 and D == P and TT > 0
    EP = E // P
    CH = 30
    NCH = EP // CH
    VC = 8
    TC = NCH - VC
    TC_EARLY = 3
    PAIR_BANKS = -(-CH // (2 * Q))
    ER = E - EP * P
    assert EP % CH == 0 and CH % 2 == 0 and 2 * DE == P

    windows_src = nc.dram_tensor("windows_src", (WR, P), i32, kind="Internal").ap()
    windows_dst = nc.dram_tensor("windows_dst", (WR, P), i32, kind="Internal").ap()
    windows_edge = nc.dram_tensor("windows_edge", (WR, P), fp32, kind="Internal").ap()
    edge_score = nc.dram_tensor("edge_score", (E,), fp32, kind="Internal").ap()
    tile_rows = nc.dram_tensor("tile_rows", (NB * P, 2 * P + 2), fp32, kind="Internal").ap()

    def overlapped(a, rows, first=0):
        return bass.AP(tensor=a.tensor, offset=first * STEP, ap=[[STEP, rows], [1, P]])

    ctx = ExitStack()
    with ctx:
        def sb(name, shape, dt=fp32):
            return ctx.enter_context(nc.sbuf_tensor(name, shape, dt))

        def pb(name):
            return ctx.enter_context(nc.psum_tensor(name, [P, 512], fp32))

        def sem(name):
            return ctx.enter_context(nc.semaphore(name))

        ident = sb("ident", [P, P])
        ones = sb("ones", [P, P])
        node_iota_i = sb("node_iota_i", [P, P], i32)
        node_iota = sb("node_iota", [P, P])
        first_i = sb("first_i", [P, NB], i32)
        first = sb("first", [P, NB])
        pivots_i = sb("pivots_i", [1, NR], i32)
        pivots = sb("pivots", [1, NR])
        src_rows = sb("src_rows", [P, RING, K, D])

        scratch = src_rows[:, 1:RING, :, :].rearrange("p r k d -> p (r k d)")
        taken = [0]

        def carve(width, dt=fp32):
            at = taken[0]
            taken[0] += NB * width
            part = scratch[:, at:at + NB * width]
            return (part if dt == fp32 else part.bitcast(dt)).rearrange("p (b n) -> p b n", b=NB)

        runs = carve(RUN, i32)
        below = carve(max(NR, RUN))
        win_src = carve(P, i32)
        win_dst = carve(P, i32)
        src_f = carve(P)
        rel = carve(P)
        in_tile = carve(P)
        hit = carve(P)
        desc = carve(P)
        count = sb("count", [P, NB])
        run_f = sb("run_f", [P, NB])
        run_i = sb("run_i", [P, NB], i32)
        start_f = sb("start_f", [P, NB])
        start_i = sb("start_i", [P, NB], i32)
        start_r = sb("start_r", [P, NB], i32)
        start_k = sb("start_k", [P, NB], i32)
        win_edge = sb("win_edge", [P, NB, P])
        same = sb("same", [P, NB, P + 2])
        tally = sb("tally", [P, 2])
        verdict = sb("verdict", [1, 2])
        regular = sb("regular", [1, 1], i32)
        src_cols = sb("src_cols", [P, NB, P], i32)
        rel_cols = sb("rel_cols", [P, NB * P])
        wn = sb("wn", [P, D])
        we2 = sb("we2", [P, 2, DE])
        wa = sb("wa", [P, 3])
        wn_t = sb("wn_t", [D, P])
        v_src = sb("v_src", [P, D])
        v_dst = sb("v_dst", [D, P])
        v_edge = sb("v_edge", [P, DE])
        v_dst_row = sb("v_dst_row", [P, D])
        v_edge2 = sb("v_edge2", [P, 2])
        edge_rest = sb("edge_rest", [P, DE])
        score = sb("score", [P, EP])
        score_rest = sb("score_rest", [P, 1])

        x_ring = sb("x_ring", [P, RING, K, D])
        edge_v_in, edge_t_in = (x_ring[:, r, :, :].rearrange("p k d -> p (k d)")[:, 0:2 * CH * DE].rearrange(
            "p (c t d) -> p c t d", c=2, d=DE) for r in (2, 3))
        rows_ring = sb("rows_ring", [K, RING, 2 * P + 2])
        index_ring = sb("index_ring", [P, RING, K], i32)
        rel_ring = sb("rel_ring", [P, RING, K])
        a_cols = sb("a_cols", [P, RING, K])
        b_cols = sb("b_cols", [P, RING, K])
        ab_cols = sb("ab_cols", [P, RING, K])
        w_cols = sb("w_cols", [P, RING, K])
        x_t = sb("x_t", [D, 2, Q * P])
        select = sb("select", [P, 2, Q * P])
        gather_t = sb("gather_t", [D, 2, Q * P])
        junk_a = sb("junk_a", [P, 4, Q, D], mybir.dt.bfloat16)
        junk_b = sb("junk_b", [P, 4, Q, P], mybir.dt.bfloat16)
        pen = sb("pen", [K, P + 1])
        zt = sb("zt", [K, P])
        z = sb("z", [K, P])
        m_run = sb("m_run", [K, P])
        m_seg = sb("m_seg", [K, P])
        z_sub = sb("z_sub", [K, P])
        ex = sb("ex", [K, P])
        s_run = sb("s_run", [K, P])
        s_seg = sb("s_seg", [K, P])
        s_inv = sb("s_inv", [K, P])
        alpha = sb("alpha", [K, P])
        bn6 = sb("bn6", [P, RING, K, 6])
        mean2 = sb("mean2", [P, K])
        mean_gap = sb("mean_gap", [P, K])
        moment = sb("moment", [P, K])
        gap_sq = sb("gap_sq", [P, K])
        moment_eps = sb("moment_eps", [P, K])
        minus_mean = sb("minus_mean", [P, K])
        var_eps = sb("var_eps", [P, K])
        half_bits = sb("half_bits", [P, K], i32)
        guess = sb("guess", [P, 1, K], i32)
        root = sb("root", [P, NEWTON, K])
        square = sb("square", [P, NEWTON, K])
        error = sb("error", [P, NEWTON, K])
        rstd = sb("rstd", [P, RING, K])
        shift = sb("shift", [P, RING, K])

        xt_bank = pb("xt_bank")
        b_bank = [pb(f"b_bank{i}") for i in range(2)]
        g_bank = [pb(f"g_bank{i}") for i in range(2)]
        y_bank = [pb(f"y_bank{i}") for i in range(2)]
        row_bank = pb("row_bank")

        weights_in = sem("weights_in")
        weights_ps = sem("weights_ps")
        weights_sb = sem("weights_sb")
        edge_v_arrived = [sem(f"edge_v_arrived{i}") for i in range(2)]
        edge_t_arrived = [sem(f"edge_t_arrived{i}") for i in range(2)]
        edge_v_used = sem("edge_v_used")
        edge_rest_in = sem("edge_rest_in")
        pairs_ps = sem("pairs_ps")
        pairs_sb = sem("pairs_sb")
        score_ps = sem("score_ps")
        v_edge2_zero = sem("v_edge2_zero")
        score_ready = sem("score_ready")
        score_out = sem("score_out")
        table_out = sem("table_out")
        same_out = sem("same_out")
        win_edge_in = sem("win_edge_in")
        x_in = [[sem(f"x_in{i}_{c}") for c in range(K // XL)] for i in range(RING)]
        x_zero = sem("x_zero")
        rows_in = [sem(f"rows_in{i}") for i in range(RING)]
        src_in = [[sem(f"src_in{i}_{q}") for q in range(QG)] for i in range(RING)]
        index_ready = sem("index_ready")
        rel_copied = sem("rel_copied")
        xt_ps = sem("xt_ps")
        xt_sb = sem("xt_sb")
        b_ready = sem("b_ready")
        cols_done = sem("cols_done")
        sel_ready = sem("sel_ready")
        g_ps = sem("g_ps")
        g_sb = sem("g_sb")
        y_ps = sem("y_ps")
        rstd_ready = sem("rstd_ready")
        normed = sem("normed")
        y_sb = sem("y_sb")
        stored = [[sem(f"stored{i}_{c}") for c in range(K // XL)] for i in range(RING)]
        ab_ready = sem("ab_ready")
        ab_row = sem("ab_row")
        rowstep = sem("rowstep")
        ROWSTEPS = 8
        FINISHSTEPS = 5 + 3 * NEWTON
        sub_ready = sem("sub_ready")
        ex_ready = sem("ex_ready")
        alpha_ready = sem("alpha_ready")
        alpha_col = sem("alpha_col")
        w_ready = sem("w_ready")
        stats_done = sem("stats_done")
        finish_step = sem("finish_step")

        def at_least(eng, sem, value):
            if not isinstance(value, int) or value > 0:
                eng.wait_ge(sem, value)

        class Group:
            def __init__(self, i, slot):
                self.i, self.slot = i, slot
                self.n = i * RING + slot
                self.tail = isinstance(i, int) and self.n == GF
                self.sizes = [min(Q, TT - Q * s) for s in range(TQ)] if self.tail else [Q] * QG
                self.tiles = sum(self.sizes)
                self.first = isinstance(i, int) and self.n == 0

            def exists(self):
                return not isinstance(self.i, int) or self.n <= GF

            def after(self, k):
                s = self.slot + k
                return Group(self.i + s // RING, s % RING)

        TAIL = Group(GF // RING, GF % RING)

        def over_groups(eng, body):
            for n in range(RING):
                body(Group(0, n))
            with eng.Fori(1, LOOPS) as i:
                for slot in range(RING):
                    body(Group(i, slot))
            for n in range(LOOPS * RING, GF + 1):
                body(Group(n // RING, n % RING))

        def chunks(g):
            return -(-g.tiles // XL)

        def load_x(sp, g, c):
            k = c * XL
            ragged = g.tail and c == chunks(g) - 1
            m = min(XL, g.tiles - k) - ragged
            sp.dma_start(x_ring[:, g.slot, k:k + m, :],
                         x[bass.ds(g.n * (K * P) + k * P, m * P), :].rearrange("(k p) d -> p k d", p=P)
                         ).then_inc(x_in[g.slot][c], 16)
            if ragged:
                sp.wait_ge(x_zero, 1)
                sp.dma_start(x_ring[0:LAST, g.slot, k + m, :], x[N - LAST:N, :]).then_inc(x_in[g.slot][c], 16)

        def gather(pool, g, s):
            if s == 0:
                nc.gpsimd.tensor_copy(index_ring[:, g.slot, 0:g.tiles],
                                      src_cols[:, :, :].rearrange("p b q -> p (b q)")[:, bass.ds(g.n * K, g.tiles)]
                                      ).then_inc(index_ready, 1)
                pool.wait_ge(index_ready, g.n + 1)
                pool.nop(nofuse=True)
            for k in range(s * Q, s * Q + g.sizes[s]):
                pool.indirect_dma_start(
                    out=src_rows[:, g.slot, k, :], out_offset=None, in_=x[:, :],
                    in_offset=bass.IndirectOffsetOnAxis(ap=index_ring[:, g.slot, k:k + 1], axis=0)
                ).then_inc(src_in[g.slot][s], 16)

        pivots_in = sem("pivots_in")
        tables_out = sem("tables_out")
        iotas = sem("iotas")
        consts = sem("consts")
        dve = sem("dve")
        pivots_bc = sem("pivots_bc")
        run_ready = sem("run_ready")
        runs_in = sem("runs_in")
        start_ready = sem("start_ready")
        win_src_in = sem("win_src_in")
        win_dst_in = sem("win_dst_in")
        src_f_ready = sem("src_f_ready")
        rel_ready = sem("rel_ready")
        cols_ps = sem("cols_ps")
        cols_sb = sem("cols_sb")
        tally_ready = sem("tally_ready")
        tally_ps = sem("tally_ps")

        edge_v = edge[0:EP * P, :].rearrange("(p t) d -> p t d", t=EP)

        with nc.Block() as block:
            @block.sync
            def _(sp):
                sp.dma_start(pivots_i[:, :], dst.rearrange("(a b) -> b a", b=RUN)[0:1, :],
                             allow_slow_non_contiguous=True).then_inc(pivots_in, 16)
                for to, a in ((wn[:, :], Wn), (we2[:, 0, :], We), (we2[:, 1, :], We)):
                    sp.dma_start(to, a[:, :]).then_inc(weights_in, 16)
                sp.dma_start(wa[:, :], Wa.rearrange("a (k d) -> d (a k)", k=3),
                             allow_slow_non_contiguous=True).then_inc(weights_in, 16)

                def load_edge(c):
                    if c >= 2:
                        sp.wait_ge(edge_v_used, c - 1)
                    sp.dma_start(edge_v_in[:, c % 2, :, :],
                                 edge_v[:, c * CH:(c + 1) * CH, :]).then_inc(edge_v_arrived[c % 2], 16)

                load_edge(0)
                load_edge(1)
                for table, a in ((windows_src, src), (windows_dst, dst)):
                    sp.dma_start(table[0:WR16, :], overlapped(a, WR16)).then_inc(tables_out, 16)
                    sp.dma_start(table[WR16:WR, :], overlapped(a, WR - WR16, WR16)).then_inc(tables_out, 16)
                sp.dma_start(edge_rest[0:ER, :], edge[EP * P:E, :]).then_inc(edge_rest_in, 16)
                for c in range(2, VC):
                    load_edge(c)
                for k in range(K // XL):
                    load_x(sp, Group(0, 0), k)
                sp.wait_ge(score_ready, 2)
                sp.dma_start(edge_score[0:EP * P].rearrange("(p t) -> p t", t=EP), score[:, :]).then_inc(score_out, 16)
                sp.dma_start(edge_score[EP * P:E].rearrange("(p t) -> p t", t=1), score_rest[0:ER, :]).then_inc(score_out, 16)
                sp.wait_ge(score_out, 32)
                sp.dma_start(windows_edge[0:WR16, :], overlapped(edge_score, WR16)).then_inc(table_out, 16)
                sp.dma_start(windows_edge[WR16:WR, :], overlapped(edge_score, WR - WR16, WR16)).then_inc(table_out, 16)
                sp.wait_ge(tables_out, 64)
                for k in range(K // XL):
                    sp.wait_ge(x_in[0][k], 16)

            @block.gpsimd
            def _(pool):
                nc.gpsimd.iota(first_i[:, :], pattern=[[P * P, NB]], base=0, channel_multiplier=P).then_inc(iotas, 1)
                nc.gpsimd.iota(node_iota_i[:, :], pattern=[[1, P]], base=0, channel_multiplier=0).then_inc(iotas, 1)
                nc.gpsimd.memset(ident[:, :], 0.0).then_inc(iotas, 1)
                pool.wait_ge(iotas, 3)
                nc.gpsimd.affine_select(out=ident[:, :], in_=ident[:, :], compare_op=ALU.not_equal, fill=1.0,
                                        base=0, pattern=[[-1, P]], channel_multiplier=1).then_inc(iotas, 1)
                pool.wait_ge(run_ready, 1)
                for b in range(NB):
                    pool.indirect_dma_start(
                        out=runs[:, b, :], out_offset=None, in_=dst.rearrange("(a b) -> a b", b=RUN),
                        in_offset=bass.IndirectOffsetOnAxis(ap=run_i[:, b:b + 1], axis=0)).then_inc(runs_in, 16)
                pool.wait_ge(start_ready, 1)
                pool.wait_ge(tables_out, 64)
                for table, win, arrived in ((windows_src, win_src, win_src_in), (windows_dst, win_dst, win_dst_in)):
                    for b in range(NB):
                        pool.indirect_dma_start(
                            out=win[:, b, :], out_offset=None, in_=table[:, :],
                            in_offset=bass.IndirectOffsetOnAxis(ap=start_k[:, b:b + 1], axis=0)).then_inc(arrived, 16)
                pool.wait_ge(cols_sb, NB)
                for s in range(QG):
                    gather(pool, Group(0, 0), s)

            @block.tensor
            def _(pe):
                pe.wait_ge(consts, 1)
                nc.tensor.matmul(row_bank[:, 0:NR], ones[0:1, :], pivots[0:1, :], start=True, stop=True).then_inc(pivots_bc, 1)
                pe.wait_ge(iotas, 4)
                pe.wait_ge(weights_in, 64)
                nc.tensor.transpose(g_bank[0][:, 0:P], wn[:, :], ident[:, :])
                for bank, w, a, b in ((g_bank[1], D, wa[:, 0:1].to_broadcast([P, P]), wn[:, :]),
                                      (y_bank[0], P, wn[:, :], wa[:, 1:2].to_broadcast([P, P])),
                                      (y_bank[1], DE, wa[:, 2:3].to_broadcast([P, P]), we2[:, 0, :]),
                                      (xt_bank, D, wa[:, 1:2].to_broadcast([P, P]), wn[:, :]),
                                      (b_bank[0], 1, we2[:, :, :].rearrange("p r d -> p (r d)"), wa[:, 2:3])):
                    last = nc.tensor.matmul(bank[:, 0:w], a, b, start=True, stop=True)
                last.then_inc(weights_ps, 1)
                pe.wait_ge(weights_sb, 1)

                def edge_chunk(c):
                    pe.wait_ge(edge_t_arrived[c % 2], 16 * (c // 2 + 1))
                    for b in range(PAIR_BANKS):
                        n = c * PAIR_BANKS + b
                        pairs = min(Q, CH // 2 - b * Q)
                        if n >= 2:
                            pe.wait_ge(pairs_sb, n - 1)
                        for k in range(pairs):
                            u = b * Q + k
                            last = nc.tensor.transpose(
                                (xt_bank, b_bank[0])[n % 2][:, k * P:(k + 1) * P],
                                edge_t_in[:, c % 2, 2 * u:2 * u + 2, :].rearrange("p t d -> p (t d)"), ident[:, :])
                        last.then_inc(pairs_ps, 1)
                        if n >= 1:
                            edge_dots(n - 1)

                def edge_dots(n):
                    c, b = divmod(n, PAIR_BANKS)
                    pe.wait_ge(pairs_sb, n + 1)
                    for k in range(min(Q, CH // 2 - b * Q)):
                        at = c * CH + 2 * (b * Q + k)
                        last = nc.tensor.matmul(b_bank[1][:, at:at + 2], x_t[:, n % 2, k * P:(k + 1) * P],
                                                v_edge2[:, :], start=True, stop=True)
                    last.then_inc(score_ps, 1)

                for c in range(TC_EARLY):
                    edge_chunk(c)
                n = 0
                for ready, rows in ((src_f_ready, src_f), (rel_ready, rel)):
                    pe.wait_ge(ready, 1)
                    for b in range(NB):
                        if n >= 4:
                            pe.wait_ge(cols_sb, n - 3)
                        bank = (g_bank + y_bank)[n % 4]
                        nc.tensor.transpose(bank[:, 0:P], rows[:, b, :], ident[:, :]).then_inc(cols_ps, 1)
                        n += 1
                for c in range(TC_EARLY, TC):
                    edge_chunk(c)
                edge_dots(TC * PAIR_BANKS - 1)
                pe.wait_ge(tally_ready, 1)
                nc.tensor.matmul(row_bank[0:1, 0:2], ones[:, 0:1], tally[:, :], start=True, stop=True).then_inc(tally_ps, 1)

            @block.scalar
            def _(act):
                def load_edge(c):
                    act.dma_start(edge_t_in[:, c % 2, :, :], edge_v[:, (VC + c) * CH:(VC + c + 1) * CH, :]
                                  ).then_inc(edge_t_arrived[c % 2], 16)

                load_edge(0)
                load_edge(1)
                act.wait_ge(weights_ps, 1)
                act.wait_ge(v_edge2_zero, 1)
                for to, bank, w in ((wn_t, g_bank[0], P), (v_src, g_bank[1], D), (v_dst, y_bank[0], P),
                                    (v_edge, y_bank[1], DE), (v_dst_row, xt_bank, D)):
                    nc.scalar.activation(to[:, :], bank[:, 0:w], ACT.Copy)
                for r in range(2):
                    last = nc.scalar.activation(v_edge2[r * DE:(r + 1) * DE, r:r + 1],
                                                b_bank[0][r * DE:(r + 1) * DE, 0:1], ACT.Copy)
                last.then_inc(weights_sb, 1)

                def pairs_leave(c):
                    for b in range(PAIR_BANKS):
                        n = c * PAIR_BANKS + b
                        w = min(Q, CH // 2 - b * Q) * P
                        act.wait_ge(pairs_ps, n + 1)
                        if n >= 2:
                            act.wait_ge(score_ps, n - 1)
                        nc.scalar.activation(x_t[:, n % 2, 0:w], (xt_bank, b_bank[0])[n % 2][:, 0:w],
                                             ACT.Copy).then_inc(pairs_sb, 1)
                    if c + 2 < TC:
                        load_edge(c + 2)

                for c in range(TC_EARLY):
                    pairs_leave(c)
                for n in range(2 * NB):
                    act.wait_ge(cols_ps, n + 1)
                    bank = (g_bank + y_bank)[n % 4]
                    to = src_cols[:, n, :] if n < NB else rel_cols[:, (n - NB) * P:(n - NB + 1) * P]
                    nc.scalar.activation(to, bank[:, 0:P], ACT.Copy).then_inc(cols_sb, 1)
                for c in range(TC_EARLY, TC):
                    pairs_leave(c)
                act.wait_ge(score_ps, TC * PAIR_BANKS)
                nc.scalar.activation(score[:, VC * CH:EP], b_bank[1][:, 0:TC * CH], ACT.Copy).then_inc(score_ready, 1)

            @block.vector
            def _(v):
                steps = [0]

                def chain(ins):
                    steps[0] += 1
                    ins.then_inc(dve, 1)
                    v.wait_ge(dve, steps[0])

                def edge_chunk(c):
                    now = edge_v_in[:, c % 2, :, :]
                    v.wait_ge(edge_v_arrived[c % 2], 16 * (c // 2 + 1))
                    chain(nc.vector.tensor_tensor(
                        now, now, v_edge[:, :].rearrange("p (t d) -> p t d", t=1).to_broadcast([P, CH, DE]), ALU.mult))
                    nc.vector.tensor_reduce(score[:, c * CH:(c + 1) * CH], now, axis=AX.X, op=ALU.add).then_inc(edge_v_used, 1)

                nc.vector.memset(v_edge2[:, :], 0.0).then_inc(v_edge2_zero, 1)
                nc.vector.memset(ones[:, :], 1.0)
                v.wait_ge(pivots_in, 16)
                nc.vector.tensor_copy(pivots[:, :], pivots_i[:, :]).then_inc(consts, 1)
                v.wait_ge(iotas, 2)
                nc.vector.tensor_copy(node_iota[:, :], node_iota_i[:, :])
                chain(nc.vector.tensor_copy(first[:, :], first_i[:, :]))
                v.wait_ge(weights_sb, 1)
                edge_chunk(0)
                v.wait_ge(pivots_bc, 1)
                chain(nc.vector.tensor_tensor(
                    below[:, :, 0:NR], row_bank[:, 0:NR].rearrange("p (b n) -> p b n", b=1).to_broadcast([P, NB, NR]),
                    first[:, :].rearrange("p (b n) -> p b n", n=1).to_broadcast([P, NB, NR]), ALU.is_lt))
                chain(nc.vector.tensor_reduce(count[:, :], below[:, :, 0:NR], axis=AX.X, op=ALU.add))
                chain(nc.vector.tensor_scalar(run_f[:, :], count[:, :], -1.0, 0.0, ALU.add, ALU.max))
                nc.vector.tensor_copy(run_i[:, :], run_f[:, :]).then_inc(run_ready, 1)
                for c in (1, 2):
                    edge_chunk(c)
                v.wait_ge(runs_in, 16 * NB)
                chain(nc.vector.tensor_tensor(
                    below[:, :, 0:RUN], runs[:, :, :],
                    first[:, :].rearrange("p (b n) -> p b n", n=1).to_broadcast([P, NB, RUN]), ALU.is_lt))
                chain(nc.vector.tensor_reduce(count[:, :], below[:, :, 0:RUN], axis=AX.X, op=ALU.add))
                chain(nc.vector.scalar_tensor_tensor(out=start_f[:, :], in0=run_f[:, :], scalar=float(RUN),
                                                     in1=count[:, :], op0=ALU.mult, op1=ALU.add))
                chain(nc.vector.tensor_copy(start_i[:, :], start_f[:, :]))
                shift_bits = STEP.bit_length() - 1
                chain(nc.vector.tensor_single_scalar(start_r[:, :], start_i[:, :], shift_bits, op=ALU.arith_shift_right))
                nc.vector.tensor_single_scalar(start_k[:, :], start_r[:, :], float(WR - 1), op=ALU.min).then_inc(start_ready, 1)
                edge_chunk(3)
                v.wait_ge(win_src_in, 16 * NB)
                nc.vector.tensor_copy(src_f[:, :, :], win_src[:, :, :]).then_inc(src_f_ready, 1)
                v.wait_ge(win_dst_in, 16 * NB)
                nc.vector.tensor_tensor(
                    rel[:, :, :], win_dst[:, :, :],
                    first[:, :].rearrange("p (b n) -> p b n", n=1).to_broadcast([P, NB, P]), ALU.subtract).then_inc(rel_ready, 1)
                v.wait_ge(rel_ready, 1)
                nc.vector.memset(same[:, :, 0:P + 2], 0.0)
                chain(nc.vector.tensor_single_scalar(in_tile[:, :, :], rel[:, :, :], 0.0, op=ALU.is_ge))
                chain(nc.vector.tensor_tensor(same[:, :, 1:P], rel[:, :, 1:P], rel[:, :, 0:P - 1], ALU.is_equal))
                chain(nc.vector.tensor_tensor(desc[:, :, 1:P], rel[:, :, 1:P], rel[:, :, 0:P - 1], ALU.is_lt))
                chain(nc.vector.scalar_tensor_tensor(out=hit[:, :, :], in0=rel[:, :, :], scalar=float(P),
                                                     in1=in_tile[:, :, :], op0=ALU.is_lt, op1=ALU.mult))
                nc.vector.tensor_reduce(tally[:, 0:1], hit[:, :, :], axis=AX.XY, op=ALU.add)
                nc.vector.tensor_reduce(tally[:, 1:2], desc[:, :, 1:P], axis=AX.XY, op=ALU.add).then_inc(tally_ready, 1)
                for c in range(4, VC):
                    edge_chunk(c)
                v.wait_ge(edge_rest_in, 16)
                nc.vector.tensor_tensor_reduce(out=junk_a[0:ER, 0, 0, 0:DE], in0=edge_rest[0:ER, :], in1=v_edge[0:ER, :],
                                               scale=1.0, scalar=0.0, op0=ALU.mult, op1=ALU.add,
                                               accum_out=score_rest[0:ER, :]).then_inc(score_ready, 1)
                v.wait_ge(edge_v_used, VC)
                v.wait_ge(tally_ps, 1)
                chain(nc.vector.tensor_copy(verdict[:, :], row_bank[0:1, 0:2]))
                chain(nc.vector.tensor_single_scalar(verdict[:, 1:2], verdict[:, 1:2], 0.0, op=ALU.is_equal))
                chain(nc.vector.scalar_tensor_tensor(out=regular[:, :], in0=verdict[:, 0:1], scalar=float(E),
                                                     in1=verdict[:, 1:2], op0=ALU.is_equal, op1=ALU.mult))

        def load_rows(sp, g):
            sp.dma_start(rows_ring[:, g.slot, :], tile_rows[bass.ds(g.n * K, K), :]).then_inc(rows_in[g.slot], 16)

        def chunk_count(g, c):
            return (g.i + 1) * 16 + (16 if g.tail and c == chunks(g) - 1 else 0)

        def fast_sync(sp):
            tile_v = tile_rows.rearrange("(b p) c -> p b c", p=P)
            sp.dma_start(tile_v[:, :, 0:P + 2], same[:, :, :]).then_inc(same_out, 16)
            for n in (1, 2):
                for k in range(K // XL):
                    load_x(sp, Group(0, n), k)
            sp.wait_ge(win_edge_in, 16 * NB)
            sp.dma_start(tile_v[:, :, P + 2:2 * P + 2], win_edge[:, :, :]).then_inc(same_out, 16)
            sp.wait_ge(same_out, 32)
            for n in range(3):
                load_rows(sp, Group(0, n))

            def store(g, c):
                sp.wait_ge(normed, QG * g.n + min(2 * c + 2, len(g.sizes)))
                k = c * XL
                ragged = g.tail and c == chunks(g) - 1
                m = min(XL, g.tiles - k) - ragged
                sp.dma_start(out[bass.ds(g.n * (K * P) + k * P, m * P), :].rearrange("(k p) d -> p k d", p=P),
                             x_ring[:, g.slot, k:k + m, :]).then_inc(stored[g.slot][c], 16)
                if ragged:
                    sp.dma_start(out[N - LAST:N, :], x_ring[0:LAST, g.slot, k + m, :]).then_inc(stored[g.slot][c], 16)

            def body(g):
                last, ahead = g.after(-1), g.after(3)
                if ahead.exists():
                    at_least(sp, alpha_ready, g.n)
                    load_rows(sp, ahead)
                for c in range(K // XL):
                    if not g.first:
                        store(last, c)
                    if ahead.exists() and c < chunks(ahead):
                        if not g.first:
                            sp.wait_ge(stored[last.slot][c], chunk_count(last, c))
                        load_x(sp, ahead, c)

            over_groups(sp, body)
            for c in range(chunks(TAIL)):
                store(TAIL, c)
            for slot in range(RING):
                for c in range(K // XL):
                    tail = slot == TAIL.slot and c < chunks(TAIL)
                    sp.wait_ge(stored[slot][c], chunk_count(TAIL, c) if tail else 16 * len(range(slot, GF, RING)))

        def fast_gpsimd(pool):
            for n in (1, 2):
                for s in range(QG):
                    gather(pool, Group(0, n), s)
                    if n == 1 and s == 3:
                        pool.wait_ge(table_out, 32)
                        for b in range(NB):
                            pool.indirect_dma_start(
                                out=win_edge[:, b, :], out_offset=None, in_=windows_edge[:, :],
                                in_offset=bass.IndirectOffsetOnAxis(ap=start_k[:, b:b + 1], axis=0)).then_inc(win_edge_in, 16)

            def body(g):
                ahead = g.after(3)
                if ahead.exists():
                    at_least(pool, g_ps, QG * g.n)
                    if ahead.tail:
                        c = chunks(ahead) - 1
                        pool.wait_ge(stored[ahead.slot][c], chunk_count(g.after(-1), c))
                        nc.gpsimd.memset(x_ring[:, ahead.slot, ahead.tiles - 1, :], 0.0).then_inc(x_zero, 1)
                    for s in range(len(ahead.sizes)):
                        gather(pool, ahead, s)

            over_groups(pool, body)

        def has_a(g, s):
            ahead = g.after(2)
            return (ahead, s) if ahead.exists() and s < len(ahead.sizes) else None

        def has_b(g, s):
            ahead = g.after(2) if s else g.after(1)
            q = s - 1 if s else QG - 1
            if s == 0 and g.first:
                return None
            return (ahead, q) if ahead.exists() and q < len(ahead.sizes) else None

        def back(g, s, k):
            if s >= k:
                return g, s - k
            return None if g.first else (g.after(-1), s - k + QG)

        AB_AT, ROWS_AT, MAX_AT, SUM_AT, COLS_AT = 0, 1, 3, 5, 6
        RSTD_AT = 2
        NORM_AT = {3: (0,), 4: (1, 2), 5: (3, 4), 6: (5, 6), 7: (7,)}

        def pe_transpose(pe, g, q):
            n = QG * g.n + q
            if q * Q % XL == 0:
                pe.wait_ge(x_in[g.slot][q * Q // XL], chunk_count(g, q * Q // XL))
            at_least(pe, xt_sb, n)
            for k in range(g.sizes[q]):
                last = nc.tensor.transpose(xt_bank[:, k * P:(k + 1) * P], x_ring[:, g.slot, q * Q + k, :], ident[:, :])
            last.then_inc(xt_ps, 1)

        def pe_b(pe, g, q):
            n = QG * g.n + q
            w = g.sizes[q] * P
            at_least(pe, xt_sb, n + 1)
            at_least(pe, cols_done, n - 1)
            nc.tensor.matmul(b_bank[q % 2][:, 0:w], v_dst[:, :], x_t[:, q % 2, 0:w], start=True, stop=True).then_inc(b_ready, 1)

        def act_xt(act, g, q):
            n = QG * g.n + q
            w = g.sizes[q] * P
            act.wait_ge(xt_ps, n + 1)
            at_least(act, b_ready, n - 1)
            nc.scalar.activation(x_t[:, q % 2, 0:w], xt_bank[:, 0:w], ACT.Copy).then_inc(xt_sb, 1)

        def dve_a(v, g, q):
            if q == 0:
                nc.vector.tensor_copy(rel_ring[:, g.slot, 0:g.tiles],
                                      rel_cols[:, bass.ds(g.n * K, g.tiles)]).then_inc(rel_copied, 1)
                v.wait_ge(rel_copied, g.n + 1)
            v.wait_ge(src_in[g.slot][q], (g.i + 1) * 64 if not g.tail else g.i * 64 + 16 * g.sizes[q])
            for k in range(q * Q, q * Q + g.sizes[q]):
                nc.vector.tensor_tensor_reduce(out=junk_a[:, q % 4, k % Q, :], in0=src_rows[:, g.slot, k, :], in1=v_src[:, :],
                                               scale=1.0, scalar=0.0, op0=ALU.mult, op1=ALU.add,
                                               accum_out=a_cols[:, g.slot, k:k + 1])

        def dve_b(v, g, q):
            v.wait_ge(b_ready, QG * g.n + q + 1)
            for k in range(q * Q, q * Q + g.sizes[q]):
                j = k - q * Q
                last = nc.vector.scalar_tensor_tensor(
                    out=junk_b[:, q % 4, k % Q, :], in0=node_iota[:, :], scalar=rel_ring[:, g.slot, k:k + 1],
                    in1=b_bank[q % 2][:, j * P:(j + 1) * P], op0=ALU.is_equal, op1=ALU.mult,
                    accum_out=b_cols[:, g.slot, k:k + 1])
            last.then_inc(cols_done, 1)

        def dve_ab(v, g):
            at_least(v, cols_done, QG * g.n + len(g.sizes))
            t = g.tiles
            nc.vector.tensor_tensor(ab_cols[:, g.slot, 0:t], a_cols[:, g.slot, 0:t], b_cols[:, g.slot, 0:t],
                                    ALU.add).then_inc(ab_ready, 1)

        def pe_ab_rows(pe, g):
            pe.wait_ge(ab_ready, g.n + 1)
            nc.tensor.transpose(row_bank[0:g.tiles, 0:P], ab_cols[:, g.slot, 0:g.tiles], ident[:, :]).then_inc(ab_row, 1)

        def dve_rows_max(v, g):
            t = g.tiles
            base = ROWSTEPS * g.n
            kept = rows_ring[0:t, g.slot, 0:P + 1]
            v.wait_ge(rows_in[g.slot], (g.i + 1) * 16)
            nc.vector.tensor_scalar(pen[0:t, :], kept, -1.0, BIG, ALU.add, ALU.mult)
            v.wait_ge(ab_row, g.n + 1)
            nc.vector.tensor_tensor(zt[0:t, :], row_bank[0:t, 0:P], rows_ring[0:t, g.slot, P + 2:2 * P + 2],
                                    ALU.add).then_inc(rowstep, 1)
            v.wait_ge(rowstep, base + 1)
            nc.vector.scalar_tensor_tensor(out=z[0:t, :], in0=zt[0:t, :], scalar=SLOPE, in1=zt[0:t, :],
                                           op0=ALU.mult, op1=ALU.max).then_inc(rowstep, 1)
            v.wait_ge(rowstep, base + 2)
            nc.vector.tensor_tensor_scan(m_run[0:t, :], pen[0:t, 0:P], z[0:t, :], 0.0, ALU.add, ALU.max).then_inc(rowstep, 1)
            v.wait_ge(rowstep, base + 3)
            nc.vector.tensor_tensor_scan(m_seg[0:t, ::-1], pen[0:t, P:0:-1], m_run[0:t, ::-1], 0.0,
                                         ALU.add, ALU.max).then_inc(rowstep, 1)
            v.wait_ge(rowstep, base + 4)
            nc.vector.tensor_tensor(z_sub[0:t, :], z[0:t, :], m_seg[0:t, :], ALU.subtract).then_inc(sub_ready, 1)

        def act_exp(act, g):
            act.wait_ge(sub_ready, g.n + 1)
            nc.scalar.activation(ex[0:g.tiles, :], z_sub[0:g.tiles, :], ACT.Exp).then_inc(ex_ready, 1)

        def dve_rows_sum(v, g):
            t = g.tiles
            base = ROWSTEPS * g.n
            v.wait_ge(ex_ready, g.n + 1)
            nc.vector.tensor_tensor_scan(s_run[0:t, :], rows_ring[0:t, g.slot, 0:P], ex[0:t, :], 0.0,
                                         ALU.mult, ALU.add).then_inc(rowstep, 1)
            v.wait_ge(rowstep, base + 5)
            nc.vector.tensor_tensor_scan(s_seg[0:t, ::-1], rows_ring[0:t, g.slot, P:0:-1], s_run[0:t, ::-1], 0.0,
                                         ALU.mult, ALU.max).then_inc(rowstep, 1)
            v.wait_ge(rowstep, base + 6)
            nc.vector.scalar_tensor_tensor(out=s_run[0:t, :], in0=s_seg[0:t, :], scalar=0.0, in1=s_seg[0:t, :],
                                           op0=ALU.is_equal, op1=ALU.add).then_inc(rowstep, 1)
            v.wait_ge(rowstep, base + 7)
            nc.vector.reciprocal(s_inv[0:t, :], s_run[0:t, :]).then_inc(rowstep, 1)
            v.wait_ge(rowstep, base + 8)
            nc.vector.tensor_tensor(alpha[0:t, :], ex[0:t, :], s_inv[0:t, :], ALU.mult).then_inc(alpha_ready, 1)

        def pe_alpha_cols(pe, g):
            at_least(pe, alpha_ready, g.n + 1)
            pe.nop(nofuse=True)
            t = g.tiles
            nc.tensor.transpose(row_bank[:, 256:256 + t], alpha[0:t, :], ident[0:t, 0:t]).then_inc(alpha_col, 1)

        def act_w(act, g):
            act.wait_ge(alpha_col, g.n + 1)
            nc.scalar.activation(w_cols[:, g.slot, 0:g.tiles], row_bank[:, 256:256 + g.tiles], ACT.Copy).then_inc(w_ready, 1)

        def dve_select(v, g, s):
            n = QG * g.n + s
            at_least(v, g_ps, n - 1)
            for k in range(g.sizes[s]):
                col = s * Q + k
                last = nc.vector.tensor_scalar(
                    select[:, s % 2, k * P:(k + 1) * P], node_iota[:, :], rel_ring[:, g.slot, col:col + 1],
                    w_cols[:, g.slot, col:col + 1], ALU.is_equal, ALU.mult)
            last.then_inc(sel_ready, 1)

        def pe_gather(pe, g, s):
            n = QG * g.n + s
            pe.wait_ge(sel_ready, n + 1)
            at_least(pe, g_sb, n - 1)
            for k in range(g.sizes[s]):
                last = nc.tensor.matmul(g_bank[s % 2][:, k * P:(k + 1) * P], src_rows[:, g.slot, s * Q + k, :],
                                        select[:, s % 2, k * P:(k + 1) * P], start=True, stop=True)
            last.then_inc(g_ps, 1)

        def act_gather(act, g, s):
            n = QG * g.n + s
            w = g.sizes[s] * P
            at_least(act, g_ps, n + 1)
            at_least(act, y_ps, n - 1)
            nc.scalar.activation(gather_t[:, s % 2, 0:w], g_bank[s % 2][:, 0:w], ACT.Copy).then_inc(g_sb, 1)

        def pe_residual(pe, g, s):
            t = g.sizes[s]
            n = QG * g.n + s
            at_least(pe, y_sb, n - 1)
            nc.tensor.matmul(y_bank[s % 2][:, 0:t * D], ident[:, :],
                             x_ring[:, g.slot, s * Q:s * Q + t, :].rearrange("p k d -> p (k d)"), start=True, stop=False)

        def pe_project(pe, g, s):
            n = QG * g.n + s
            at_least(pe, g_sb, n + 1)
            t = g.sizes[s]
            for k in range(t):
                last = nc.tensor.matmul(y_bank[s % 2][:, k * D:(k + 1) * D], gather_t[:, s % 2, k * P:(k + 1) * P],
                                        wn_t[:, :], start=False, stop=(k == t - 1))
            last.then_inc(y_ps, 1)

        def dve_stats(v, g, s):
            v.wait_ge(y_sb, QG * g.n + s + 1)
            for k in range(g.sizes[s]):
                last = nc.vector.bn_stats(bn6[:, g.slot, s * Q + k, :], x_ring[:, g.slot, s * Q + k, :])
            last.then_inc(stats_done, 1)

        def act_y(act, g, s):
            t = g.sizes[s]
            act.wait_ge(y_ps, QG * g.n + s + 1)
            nc.scalar.activation(x_ring[:, g.slot, s * Q:s * Q + t, :].rearrange("p k d -> p (k d)"),
                                 y_bank[s % 2][:, 0:t * D], ACT.Copy).then_inc(y_sb, 1)

        def dve_rstd(v, g):
            t = g.tiles
            base = FINISHSTEPS * g.n
            even_mean, even_m2, odd_mean, odd_m2 = (bn6[:, g.slot, 0:t, c] for c in (1, 2, 4, 5))
            v.wait_ge(stats_done, QG * g.n + len(g.sizes))
            nc.vector.tensor_tensor(mean2[:, 0:t], even_mean, odd_mean, ALU.add)
            nc.vector.tensor_tensor(mean_gap[:, 0:t], even_mean, odd_mean, ALU.subtract)
            nc.vector.tensor_tensor(moment[:, 0:t], even_m2, odd_m2, ALU.add).then_inc(finish_step, 1)
            v.wait_ge(finish_step, base + 1)
            nc.vector.scalar_tensor_tensor(out=gap_sq[:, 0:t], in0=mean_gap[:, 0:t], scalar=0.25,
                                           in1=mean_gap[:, 0:t], op0=ALU.mult, op1=ALU.mult)
            nc.vector.tensor_scalar(moment_eps[:, 0:t], moment[:, 0:t], 1.0 / D, EPS, ALU.mult, ALU.add)
            nc.vector.tensor_scalar(minus_mean[:, 0:t], mean2[:, 0:t], -0.5, None, ALU.mult).then_inc(finish_step, 1)
            v.wait_ge(finish_step, base + 2)
            nc.vector.tensor_tensor(var_eps[:, 0:t], gap_sq[:, 0:t], moment_eps[:, 0:t], ALU.add).then_inc(finish_step, 1)
            v.wait_ge(finish_step, base + 3)
            nc.vector.tensor_single_scalar(half_bits[:, 0:t], var_eps[:, 0:t].bitcast(i32), 1,
                                           op=ALU.arith_shift_right).then_inc(finish_step, 1)
            v.wait_ge(finish_step, base + 4)
            nc.vector.tensor_scalar(guess[:, 0, 0:t], half_bits[:, 0:t], -1.0, GUESS, ALU.mult, ALU.add).then_inc(finish_step, 1)
            for r in range(NEWTON):
                old = guess[:, r, 0:t].bitcast(fp32) if r == 0 else root[:, r - 1, 0:t]
                new = rstd[:, g.slot, 0:t] if r == NEWTON - 1 else root[:, r, 0:t]
                v.wait_ge(finish_step, base + 5 + 3 * r)
                nc.vector.tensor_tensor(square[:, r, 0:t], old, old, ALU.mult).then_inc(finish_step, 1)
                v.wait_ge(finish_step, base + 6 + 3 * r)
                nc.vector.scalar_tensor_tensor(out=error[:, r, 0:t], in0=square[:, r, 0:t], scalar=-0.5,
                                               in1=var_eps[:, 0:t], op0=ALU.mult, op1=ALU.mult).then_inc(finish_step, 1)
                v.wait_ge(finish_step, base + 7 + 3 * r)
                nc.vector.scalar_tensor_tensor(out=new, in0=error[:, r, 0:t], scalar=1.5, in1=old,
                                               op0=ALU.add, op1=ALU.mult).then_inc(finish_step, 1)
            v.wait_ge(finish_step, base + FINISHSTEPS)
            nc.vector.tensor_tensor(shift[:, g.slot, 0:t], minus_mean[:, 0:t], rstd[:, g.slot, 0:t],
                                    ALU.mult).then_inc(rstd_ready, 1)

        def act_norm(act, g, s):
            if s == 0:
                act.wait_ge(y_sb, QG * g.n + len(g.sizes))
                act.wait_ge(rstd_ready, g.n + 1)
            for k in range(s * Q, s * Q + g.sizes[s]):
                last = nc.scalar.activation(x_ring[:, g.slot, k, :], x_ring[:, g.slot, k, :], ACT.Identity,
                                            scale=rstd[:, g.slot, k:k + 1], bias=shift[:, g.slot, k:k + 1])
            last.then_inc(normed, 1)

        def fast_tensor(pe):
            for n in range(2):
                for q in range(QG):
                    pe_transpose(pe, Group(0, n), q)
                    pe_b(pe, Group(0, n), q)
                if n == 0:
                    pe_ab_rows(pe, Group(0, 0))
                    pe_alpha_cols(pe, Group(0, 0))

            def body(g):
                for s in range(len(g.sizes)):
                    if has_b(g, s):
                        pe_b(pe, *has_b(g, s))
                    pe_gather(pe, g, s)
                    if has_a(g, s):
                        pe_transpose(pe, *has_a(g, s))
                    if back(g, s, 1):
                        pe_residual(pe, *back(g, s, 1))
                        pe_project(pe, *back(g, s, 1))
                    if s == ROWS_AT and g.after(1).exists():
                        pe_ab_rows(pe, g.after(1))
                    if s == COLS_AT and g.after(1).exists():
                        pe_alpha_cols(pe, g.after(1))
                if g.tail:
                    pe_residual(pe, g, TQ - 1)
                    pe_project(pe, g, TQ - 1)

            over_groups(pe, body)

        def fast_scalar(act):
            for n in range(2):
                for q in range(QG):
                    act_xt(act, Group(0, n), q)
                if n == 0:
                    act_exp(act, Group(0, 0))
                    act_w(act, Group(0, 0))

            def body(g):
                for s in range(len(g.sizes)):
                    act_gather(act, g, s)
                    if has_a(g, s):
                        act_xt(act, *has_a(g, s))
                    if back(g, s, 1):
                        act_y(act, *back(g, s, 1))
                    if not g.first and not g.tail:
                        for m in NORM_AT.get(s, ()):
                            act_norm(act, g.after(-1), m)
                    if s == MAX_AT and g.after(1).exists():
                        act_exp(act, g.after(1))
                    if s == COLS_AT and g.after(1).exists():
                        act_w(act, g.after(1))
                if g.tail:
                    act_y(act, g, TQ - 1)
                    for m in range(QG):
                        act_norm(act, g.after(-1), m)
                    for s in range(TQ):
                        act_norm(act, g, s)

            over_groups(act, body)

        def fast_vector(v):
            for n in range(2):
                for q in range(QG):
                    dve_a(v, Group(0, n), q)
                    dve_b(v, Group(0, n), q)
                if n == 0:
                    dve_ab(v, Group(0, 0))
                    dve_rows_max(v, Group(0, 0))
                    dve_rows_sum(v, Group(0, 0))
            v.wait_ge(w_ready, 1)
            dve_select(v, Group(0, 0), 0)

            def body(g):
                nxt = g.after(1)
                for s in range(len(g.sizes)):
                    if has_b(g, s):
                        dve_b(v, *has_b(g, s))
                    if s + 1 < len(g.sizes):
                        dve_select(v, g, s + 1)
                    elif nxt.exists():
                        v.wait_ge(w_ready, nxt.n + 1)
                        dve_select(v, nxt, 0)
                    if has_a(g, s):
                        dve_a(v, *has_a(g, s))
                    if nxt.exists():
                        if s == AB_AT:
                            dve_ab(v, nxt)
                        if s == MAX_AT:
                            dve_rows_max(v, nxt)
                        if s == SUM_AT:
                            dve_rows_sum(v, nxt)
                    if back(g, s, 2):
                        dve_stats(v, *back(g, s, 2))
                    if s == RSTD_AT and not g.first:
                        dve_rstd(v, g.after(-1))
                if g.tail:
                    dve_stats(v, g, TQ - 2)
                    dve_stats(v, g, TQ - 1)
                    dve_rstd(v, g)

            over_groups(v, body)

        ET = -(-E // P)
        EL = E - (ET - 1) * P
        SW = D + 2
        EDGE_STEPS, NODE_STEPS = 15, 6
        state = nc.dram_tensor("state", (N, SW), fp32, kind="Internal").ap()
        room = x_ring[:, 0:2, :, :].rearrange("p r k d -> p (r k d)")
        used = [0]

        def part(width, dt=fp32):
            at = used[0]
            used[0] += -(-width // 8) * 8
            return room[:, at:at + width] if dt == fp32 else room[:, at:at + width].bitcast(dt)

        src_col, dst_col = part(ET, i32), part(ET, i32)
        dst_col_f = part(ET)
        src_now, dst_now, scatter_to = part(1, i32), part(1, i32), part(1, i32)
        dst_now_f, first_before, scatter_f = part(1), part(1), part(1)
        blank = part(SW)
        lower = part(P)
        from_rows, to_rows, old, new = part(D), part(D), part(SW), part(SW)
        edge_now = part(DE)
        products, same_dst, before, penalty, z_pen = part(D), part(P), part(P), part(P), part(P)
        dots, z_pre, z_now, m_tile, m_new = part(3), part(1), part(1), part(1), part(1)
        deltas, exps = part(2), part(2)
        weighted = part(D + 1)
        x_now, y_now, y_out = part(D), part(D), part(D)
        s_one, s_rec, mean, stats, aggr, var_e, std, std_inv = (part(w) for w in (1, 1, D, 6, 2, 1, 1, 1))
        mean_t = part(P)

        g_set = sem("g_set")
        g_cols_in = sem("g_cols_in")
        g_blank = sem("g_blank")
        g_prep = sem("g_prep")
        g_edge_in = sem("g_edge_in")
        g_index = sem("g_index")
        g_rows_in = sem("g_rows_in")
        g_z = sem("g_z")
        g_bc = sem("g_bc")
        g_delta = sem("g_delta")
        g_exp = sem("g_exp")
        g_weighted = sem("g_weighted")
        g_sum = sem("g_sum")
        g_new = sem("g_new")
        g_scattered = sem("g_scattered")
        g_dve = sem("g_dve")
        g_state_in = sem("g_state_in")
        g_mean = sem("g_mean")
        g_mean_ps = sem("g_mean_ps")
        g_mean_t = sem("g_mean_t")
        g_h = sem("g_h")
        g_var = sem("g_var")
        g_std = sem("g_std")
        g_y = sem("g_y")
        g_stored = sem("g_stored")

        def over_edges(eng, body):
            with eng.Fori(0, ET - 1) as t:
                body(t, P)
            body(ET - 1, EL)

        def over_nodes(eng, body):
            with eng.Fori(0, NT - 1) as t:
                body(t, P)
            body(NT - 1, LAST)

        class Steps:
            def __init__(self, v, base, per_iteration):
                self.v, self.base, self.per, self.k = v, base, per_iteration, 0

            def __call__(self, ins):
                self.k += 1
                ins.then_inc(g_dve, 1)
                self.v.wait_ge(g_dve, self.base + self.k)

            def end(self):
                assert self.k == self.per, self.k

        def general_sync(sp):
            sp.wait_ge(table_out, 32)
            sp.wait_ge(g_set, 1)
            for col, a in ((src_col, src), (dst_col, dst)):
                sp.dma_start(col[:, 0:ET - 1], a[0:(ET - 1) * P].rearrange("(t p) -> p t", p=P),
                             allow_slow_non_contiguous=True).then_inc(g_cols_in, 16)
                sp.dma_start(col[0:EL, ET - 1:ET], a[(ET - 1) * P:E].rearrange("(p t) -> p t", t=1)).then_inc(g_cols_in, 16)

            def clear(t, rows):
                sp.dma_start(state[bass.ds(t * P, rows), :], blank[0:rows, :]).then_inc(g_blank, 16)
                sp.wait_ge(g_blank, 16 * (t + 1))
                sp.nop(nofuse=True)

            over_nodes(sp, clear)

            def edges(t, rows):
                sp.dma_start(edge_now[0:rows, :], edge[bass.ds(t * P, rows), :]).then_inc(g_edge_in, 16)
                sp.wait_ge(g_scattered, 16 * (t + 1))
                sp.nop(nofuse=True)

            over_edges(sp, edges)

            def nodes(t, rows):
                sp.dma_start(old[0:rows, :], state[bass.ds(t * P, rows), :]).then_inc(g_state_in, 16)
                sp.dma_start(x_now[0:rows, :], x[bass.ds(t * P, rows), :]).then_inc(g_state_in, 16)
                sp.wait_ge(g_y, t + 1)
                sp.dma_start(out[bass.ds(t * P, rows), :], y_out[0:rows, :]).then_inc(g_stored, 16)
                sp.wait_ge(g_stored, 16 * (t + 1))
                sp.nop(nofuse=True)

            over_nodes(sp, nodes)

        def general_gpsimd(pool):
            nc.gpsimd.memset(room[:, 0:used[0]], 0.0).then_inc(g_prep, 1)
            pool.wait_ge(g_prep, 1)
            nc.gpsimd.memset(dst_col_f[:, :], float(N))
            nc.gpsimd.memset(dst_col[:, :], N)
            nc.gpsimd.memset(blank[:, D + 1:SW], -BIG)
            nc.gpsimd.memset(lower[:, :], 1.0).then_inc(g_prep, 1)
            pool.wait_ge(g_prep, 2)
            nc.gpsimd.affine_select(out=lower[:, :], in_=lower[:, :], compare_op=ALU.is_ge, fill=0.0,
                                    base=-1, pattern=[[-1, P]], channel_multiplier=1).then_inc(g_set, 1)
            pool.wait_ge(g_cols_in, 64)
            pool.wait_ge(g_blank, 16 * NT)

            def edges(t, rows):
                nc.gpsimd.tensor_copy(src_now[:, :], src_col[:, bass.ds(t, 1)])
                nc.gpsimd.tensor_copy(dst_now[:, :], dst_col[:, bass.ds(t, 1)]).then_inc(g_index, 1)
                pool.wait_ge(g_index, t + 1)
                pool.nop(nofuse=True)
                for rows_sb, table, idx in ((from_rows, x, src_now), (to_rows, x, dst_now), (old, state, dst_now)):
                    pool.indirect_dma_start(
                        out=rows_sb[:, :], out_offset=None, in_=table[:, :],
                        in_offset=bass.IndirectOffsetOnAxis(ap=idx[:, 0:1], axis=0),
                        bounds_check=N - 1, oob_is_err=False).then_inc(g_rows_in, 16)
                pool.wait_ge(g_new, t + 1)
                pool.nop(nofuse=True)
                pool.indirect_dma_start(
                    out=state[:, :], out_offset=bass.IndirectOffsetOnAxis(ap=scatter_to[:, 0:1], axis=0),
                    in_=new[:, :], in_offset=None, bounds_check=N - 1, oob_is_err=False).then_inc(g_scattered, 16)
                pool.wait_ge(g_scattered, 16 * (t + 1))
                pool.nop(nofuse=True)

            over_edges(pool, edges)

        def general_tensor(pe):
            def edges(t, rows):
                pe.wait_ge(g_z, t + 1)
                nc.tensor.matmul(row_bank[:, 0:P], z_now[:, 0:1].to_broadcast([P, P]), ident[:, :], start=True, stop=True)
                nc.tensor.matmul(row_bank[:, P:2 * P], dst_now_f[:, 0:1].to_broadcast([P, P]), ident[:, :], start=True,
                                 stop=True).then_inc(g_bc, 1)
                pe.wait_ge(g_weighted, t + 1)
                nc.tensor.matmul(xt_bank[:, 0:D + 1], same_dst[:, :], weighted[:, :], start=True, stop=True).then_inc(g_sum, 1)

            over_edges(pe, edges)

            def nodes(t, rows):
                pe.wait_ge(g_mean, t + 1)
                nc.tensor.transpose(b_bank[0][:, 0:P], mean[:, :], ident[:, :]).then_inc(g_mean_ps, 1)
                pe.wait_ge(g_mean_t, t + 1)
                nc.tensor.matmul(b_bank[1][:, 0:D], mean_t[:, :], wn_t[:, :], start=True, stop=True).then_inc(g_h, 1)

            over_nodes(pe, nodes)

        def general_scalar(act):
            def edges(t, rows):
                act.wait_ge(g_delta, t + 1)
                nc.scalar.activation(exps[:, :], deltas[:, :], ACT.Exp).then_inc(g_exp, 1)

            over_edges(act, edges)

            def nodes(t, rows):
                act.wait_ge(g_mean_ps, t + 1)
                nc.scalar.activation(mean_t[:, :], b_bank[0][:, 0:P], ACT.Copy).then_inc(g_mean_t, 1)
                act.wait_ge(g_var, t + 1)
                nc.scalar.activation(std[:, :], var_e[:, :], ACT.Sqrt).then_inc(g_std, 1)

            over_nodes(act, nodes)

        def general_vector(v):
            v.wait_ge(g_cols_in, 64)
            nc.vector.tensor_copy(dst_col_f[:, :], dst_col[:, :]).then_inc(g_dve, 1)
            v.wait_ge(g_dve, 1)

            def edges(t, rows):
                step = Steps(v, 1 + EDGE_STEPS * t, EDGE_STEPS)
                nc.vector.tensor_copy(dst_now_f[:, :], dst_col_f[:, bass.ds(t, 1)])
                v.wait_ge(g_edge_in, 16 * (t + 1))
                v.wait_ge(g_rows_in, 48 * (t + 1))
                for n, (a, b, w) in enumerate(((from_rows, v_src, D), (to_rows, v_dst_row, D), (edge_now, v_edge, DE))):
                    step(nc.vector.tensor_tensor(products[:, 0:w], a[:, :], b[:, :], ALU.mult))
                    step(nc.vector.tensor_reduce(dots[:, n:n + 1], products[:, 0:w], axis=AX.X, op=ALU.add))
                step(nc.vector.tensor_reduce(z_pre[:, :], dots[:, :], axis=AX.X, op=ALU.add))
                nc.vector.scalar_tensor_tensor(out=z_now[:, :], in0=z_pre[:, :], scalar=SLOPE, in1=z_pre[:, :],
                                               op0=ALU.mult, op1=ALU.max).then_inc(g_z, 1)
                v.wait_ge(g_bc, t + 1)
                step(nc.vector.tensor_tensor(same_dst[:, :], row_bank[:, P:2 * P], dst_now_f[:, 0:1].to_broadcast([P, P]),
                                             ALU.is_equal))
                nc.vector.tensor_tensor(before[:, :], same_dst[:, :], lower[:, :], ALU.mult)
                step(nc.vector.tensor_scalar(penalty[:, :], same_dst[:, :], -1.0, BIG, ALU.add, ALU.mult))
                nc.vector.tensor_reduce(first_before[:, :], before[:, :], axis=AX.X, op=ALU.max)
                step(nc.vector.tensor_tensor(z_pen[:, :], row_bank[:, 0:P], penalty[:, :], ALU.add))
                step(nc.vector.tensor_reduce(m_tile[:, :], z_pen[:, :], axis=AX.X, op=ALU.max))
                nc.vector.scalar_tensor_tensor(out=scatter_to[:, :], in0=first_before[:, :], scalar=float(N),
                                               in1=dst_now_f[:, :], op0=ALU.mult, op1=ALU.add)
                step(nc.vector.tensor_tensor(m_new[:, :], m_tile[:, :], old[:, D + 1:SW], ALU.max))
                nc.vector.tensor_tensor(deltas[:, 0:1], z_now[:, :], m_new[:, :], ALU.subtract)
                nc.vector.tensor_copy(new[:, D + 1:SW], m_new[:, :])
                nc.vector.tensor_tensor(deltas[:, 1:2], old[:, D + 1:SW], m_new[:, :], ALU.subtract).then_inc(g_delta, 1)
                v.wait_ge(g_exp, t + 1)
                nc.vector.tensor_copy(weighted[:, D:D + 1], exps[:, 0:1])
                nc.vector.tensor_tensor(weighted[:, 0:D], from_rows[:, :], exps[:, 0:1].to_broadcast([P, D]),
                                        ALU.mult).then_inc(g_weighted, 1)
                step(nc.vector.tensor_tensor(old[:, 0:D + 1], old[:, 0:D + 1], exps[:, 1:2].to_broadcast([P, D + 1]), ALU.mult))
                v.wait_ge(g_sum, t + 1)
                step(nc.vector.tensor_tensor(new[:, 0:D + 1], xt_bank[:, 0:D + 1], old[:, 0:D + 1], ALU.add))
                step(nc.vector.tensor_copy(dots[:, 0:1], m_new[:, :]))
                nc.vector.tensor_copy(dots[:, 1:2], m_new[:, :]).then_inc(g_new, 1)
                v.wait_ge(g_scattered, 16 * (t + 1))
                step.end()

            over_edges(v, edges)

            def nodes(t, rows):
                step = Steps(v, 1 + EDGE_STEPS * ET + NODE_STEPS * t, NODE_STEPS)
                v.wait_ge(g_state_in, 32 * (t + 1))
                step(nc.vector.scalar_tensor_tensor(out=s_one[:, :], in0=old[:, D:D + 1], scalar=0.0, in1=old[:, D:D + 1],
                                                    op0=ALU.is_equal, op1=ALU.add))
                step(nc.vector.reciprocal(s_rec[:, :], s_one[:, :]))
                nc.vector.tensor_tensor(mean[:, :], old[:, 0:D], s_rec[:, 0:1].to_broadcast([P, D]), ALU.mult).then_inc(g_mean, 1)
                v.wait_ge(g_h, t + 1)
                step(nc.vector.tensor_tensor(y_now[:, :], b_bank[1][:, 0:D], x_now[:, :], ALU.add))
                step(nc.vector.bn_stats(stats[:, :], y_now[:, :]))
                v.nop(nofuse=True)
                step(nc.vector.bn_aggr(aggr[:, :], stats[:, :]))
                nc.vector.tensor_scalar(var_e[:, :], aggr[:, 1:2], EPS, None, ALU.add).then_inc(g_var, 1)
                v.wait_ge(g_std, t + 1)
                step(nc.vector.reciprocal(std_inv[:, :], std[:, :]))
                nc.vector.tensor_scalar(y_out[:, :], y_now[:, :], aggr[:, 0:1], std_inv[:, 0:1], ALU.subtract,
                                        ALU.mult).then_inc(g_y, 1)
                v.wait_ge(g_stored, 16 * (t + 1))
                step.end()

            over_nodes(v, nodes)

        with nc.Block() as block:
            @block.sync
            def _(sp):
                ok = sp.value_load(regular[0:1, 0:1], min_val=0, max_val=1)
                with sp.If(ok):
                    fast_sync(sp)
                with sp.Else():
                    general_sync(sp)

            @block.gpsimd
            def _(pool):
                ok = pool.value_load(regular[0:1, 0:1], min_val=0, max_val=1)
                with pool.If(ok):
                    fast_gpsimd(pool)
                with pool.Else():
                    general_gpsimd(pool)

            @block.tensor
            def _(pe):
                ok = pe.value_load(regular[0:1, 0:1], min_val=0, max_val=1)
                with pe.If(ok):
                    fast_tensor(pe)
                with pe.Else():
                    general_tensor(pe)

            @block.scalar
            def _(act):
                ok = act.value_load(regular[0:1, 0:1], min_val=0, max_val=1)
                with act.If(ok):
                    fast_scalar(act)
                with act.Else():
                    general_scalar(act)

            @block.vector
            def _(v):
                ok = v.value_load(regular[0:1, 0:1], min_val=0, max_val=1)
                with v.If(ok):
                    fast_vector(v)
                with v.Else():
                    general_vector(v)


_INS = ["x", "src", "dst", "edge_attr_64", "L0_gnn_Wn", "L0_gnn_We", "L0_gnn_Wa"]


def kernel(**inputs):
    import numpy as _np
    import concourse.bacc as _bacc
    from concourse import mybir as _mybir
    from concourse.bass_utils import run_bass_kernel_spmd as _run

    nc = _bacc.Bacc("TRN2", target_bir_lowering=False, num_devices=1)
    arrays, args = {}, []
    for name in _INS:
        a = _np.ascontiguousarray(inputs[name])
        arrays[f"in_{name}"] = a
        args.append(nc.dram_tensor(f"in_{name}", a.shape, _mybir.dt.from_np(a.dtype), kind="ExternalInput").ap())
    out = nc.dram_tensor("out_0", tuple(inputs["x"].shape), _mybir.dt.float32, kind="ExternalOutput").ap()
    gnn_layer(nc, *args, out)
    r = _run(nc, [arrays], core_ids=[0])
    return r.results[0]["out_0"]
```

```python
import numpy as np
import concourse.bass as bass
from concourse import mybir
from contextlib import ExitStack

fp32 = mybir.dt.float32
i32 = mybir.dt.int32
ALU = mybir.AluOpType
ACT = mybir.ActivationFunctionType
AX = mybir.AxisListType

P = 128
STEP = 16
RUN = 200
K = 32
Q = 4
QG = K // Q
XL = 8
RING = 4
BIG = 1e38
EPS = 1e-5
SLOPE = 0.2
GUESS = 1597463007.0
NEWTON = 3


def gnn_layer(nc, x, src, dst, edge, Wn, We, Wa, out):
    N, D = x.shape
    E, DE = edge.shape
    NT = -(-N // P)
    LAST = N - (NT - 1) * P
    NB = -(-NT // P)
    GF = NT // K
    TT = NT - GF * K
    TQ = -(-TT // Q)
    LOOPS = (GF - 3) // RING
    WR = (E - P) // STEP + 1
    WR16 = WR // 16 * 16
    NR = E // RUN
    assert E % RUN == 0 and E % STEP == 0 and (E - P) % STEP == 0 and D == P and TT > 0
    EP = E // P
    CH = 30
    NCH = EP // CH
    VC = 8
    TC = NCH - VC
    SRC_COLS_AT, REL_COLS_AT = 2, 3
    PAIR_BANKS = -(-CH // (2 * Q))
    ER = E - EP * P
    assert EP % CH == 0 and CH % 2 == 0 and 2 * DE == P

    windows_src = nc.dram_tensor("windows_src", (WR, P), i32, kind="Internal").ap()
    windows_dst = nc.dram_tensor("windows_dst", (WR, P), i32, kind="Internal").ap()
    windows_edge = nc.dram_tensor("windows_edge", (WR, P), fp32, kind="Internal").ap()
    edge_score = nc.dram_tensor("edge_score", (E,), fp32, kind="Internal").ap()
    tile_rows = nc.dram_tensor("tile_rows", (NB * P, 2 * P + 2), fp32, kind="Internal").ap()

    def overlapped(a, rows, first=0):
        return bass.AP(tensor=a.tensor, offset=first * STEP, ap=[[STEP, rows], [1, P]])

    ctx = ExitStack()
    with ctx:
        def sb(name, shape, dt=fp32):
            return ctx.enter_context(nc.sbuf_tensor(name, shape, dt))

        def pb(name):
            return ctx.enter_context(nc.psum_tensor(name, [P, 512], fp32))

        def sem(name):
            return ctx.enter_context(nc.semaphore(name))

        ident = sb("ident", [P, P])
        ones = sb("ones", [P, P])
        node_iota_i = sb("node_iota_i", [P, P], i32)
        node_iota = sb("node_iota", [P, P])
        first_i = sb("first_i", [P, NB], i32)
        first = sb("first", [P, NB])
        pivots_i = sb("pivots_i", [1, NR], i32)
        pivots = sb("pivots", [1, NR])
        src_rows = sb("src_rows", [P, RING, K, D])

        scratch = src_rows[:, 1:RING, :, :].rearrange("p r k d -> p (r k d)")
        taken = [0]

        def carve(width, dt=fp32):
            at = taken[0]
            taken[0] += NB * width
            part = scratch[:, at:at + NB * width]
            return (part if dt == fp32 else part.bitcast(dt)).rearrange("p (b n) -> p b n", b=NB)

        runs = carve(RUN, i32)
        below = carve(max(NR, RUN))
        win_src = carve(P, i32)
        win_dst = carve(P, i32)
        src_f = carve(P)
        rel = carve(P)
        in_tile = carve(P)
        hit = carve(P)
        desc = carve(P)
        count = sb("count", [P, NB])
        run_f = sb("run_f", [P, NB])
        run_i = sb("run_i", [P, NB], i32)
        start_f = sb("start_f", [P, NB])
        start_i = sb("start_i", [P, NB], i32)
        start_r = sb("start_r", [P, NB], i32)
        start_k = sb("start_k", [P, NB], i32)
        win_edge = sb("win_edge", [P, NB, P])
        same = sb("same", [P, NB, P + 2])
        tally = sb("tally", [P, 2])
        verdict = sb("verdict", [1, 2])
        regular = sb("regular", [1, 1], i32)
        src_cols = sb("src_cols", [P, NB, P], i32)
        rel_cols = sb("rel_cols", [P, NB * P])
        wn = sb("wn", [P, D])
        we2 = sb("we2", [P, 2, DE])
        wa = sb("wa", [P, 3])
        wn_t = sb("wn_t", [D, P])
        v_src = sb("v_src", [P, D])
        v_dst = sb("v_dst", [D, P])
        v_edge = sb("v_edge", [P, DE])
        v_dst_row = sb("v_dst_row", [P, D])
        v_edge2 = sb("v_edge2", [P, 2])
        edge_rest = sb("edge_rest", [P, DE])
        score = sb("score", [P, EP])
        score_rest = sb("score_rest", [P, 1])

        x_ring = sb("x_ring", [P, RING, K, D])
        edge_v_in, edge_t_in = (x_ring[:, r, :, :].rearrange("p k d -> p (k d)")[:, 0:2 * CH * DE].rearrange(
            "p (c t d) -> p c t d", c=2, d=DE) for r in (2, 3))
        rows_ring = sb("rows_ring", [K, RING, 2 * P + 2])
        index_ring = sb("index_ring", [P, RING, K], i32)
        rel_ring = sb("rel_ring", [P, RING, K])
        a_cols = sb("a_cols", [P, RING, K])
        b_cols = sb("b_cols", [P, RING, K])
        ab_cols = sb("ab_cols", [P, RING, K])
        w_cols = sb("w_cols", [P, RING, K])
        x_t = sb("x_t", [D, 2, Q * P])
        match = sb("match", [P, RING, QG // 2, Q * P], mybir.dt.bfloat16)
        select = sb("select", [P, 2, Q * P])
        gather_t = sb("gather_t", [D, 2, Q * P])
        junk_a = sb("junk_a", [P, 4, Q, D], mybir.dt.bfloat16)
        junk_b = sb("junk_b", [P, 4, Q, P], mybir.dt.bfloat16)
        pen = sb("pen", [K, P + 1])
        zt = sb("zt", [K, P])
        z = sb("z", [K, P])
        m_run = sb("m_run", [K, P])
        m_seg = sb("m_seg", [K, P])
        z_sub = sb("z_sub", [K, P])
        ex = sb("ex", [K, P])
        s_run = sb("s_run", [K, P])
        s_seg = sb("s_seg", [K, P])
        s_inv = sb("s_inv", [K, P])
        alpha = sb("alpha", [K, P])
        bn6 = sb("bn6", [P, RING, K, 6])
        mean2 = sb("mean2", [P, K])
        mean_gap = sb("mean_gap", [P, K])
        moment = sb("moment", [P, K])
        gap_sq = sb("gap_sq", [P, K])
        moment_eps = sb("moment_eps", [P, K])
        minus_mean = sb("minus_mean", [P, K])
        var_eps = sb("var_eps", [P, K])
        half_bits = sb("half_bits", [P, K], i32)
        guess = sb("guess", [P, 1, K], i32)
        root = sb("root", [P, NEWTON, K])
        square = sb("square", [P, NEWTON, K])
        error = sb("error", [P, NEWTON, K])
        rstd = sb("rstd", [P, RING, K])
        shift = sb("shift", [P, RING, K])

        xt_bank = pb("xt_bank")
        b_bank = [pb(f"b_bank{i}") for i in range(2)]
        g_bank = [pb(f"g_bank{i}") for i in range(2)]
        y_bank = [pb(f"y_bank{i}") for i in range(2)]
        row_bank = pb("row_bank")

        weights_in = sem("weights_in")
        weights_ps = sem("weights_ps")
        weights_sb = sem("weights_sb")
        edge_v_arrived = [sem(f"edge_v_arrived{i}") for i in range(2)]
        edge_t_arrived = [sem(f"edge_t_arrived{i}") for i in range(2)]
        edge_v_used = sem("edge_v_used")
        edge_rest_in = sem("edge_rest_in")
        pairs_ps = sem("pairs_ps")
        pairs_sb = sem("pairs_sb")
        score_ps = sem("score_ps")
        v_edge2_zero = sem("v_edge2_zero")
        score_ready = sem("score_ready")
        score_out = sem("score_out")
        table_out = sem("table_out")
        same_out = sem("same_out")
        win_edge_in = sem("win_edge_in")
        x_in = [[sem(f"x_in{i}_{c}") for c in range(K // XL)] for i in range(RING)]
        x_zero = sem("x_zero")
        rows_in = [sem(f"rows_in{i}") for i in range(RING)]
        src_in = [[sem(f"src_in{i}_{q}") for q in range(QG)] for i in range(RING)]
        index_ready = sem("index_ready")
        rel_copied = sem("rel_copied")
        xt_ps = sem("xt_ps")
        xt_sb = sem("xt_sb")
        b_ready = sem("b_ready")
        cols_done = sem("cols_done")
        match_ready = sem("match_ready")
        sel_even = sem("sel_even")
        sel_odd = sem("sel_odd")
        g_ps = sem("g_ps")
        g_sb = sem("g_sb")
        y_ps = sem("y_ps")
        rstd_ready = sem("rstd_ready")
        normed = sem("normed")
        normed_v = sem("normed_v")
        y_sb = sem("y_sb")
        stored = [[sem(f"stored{i}_{c}") for c in range(K // XL)] for i in range(RING)]
        ab_ready = sem("ab_ready")
        ab_row = sem("ab_row")
        rowstep = sem("rowstep")
        ROWSTEPS = 8
        FINISHSTEPS = 5 + 3 * NEWTON
        sub_ready = sem("sub_ready")
        ex_ready = sem("ex_ready")
        alpha_ready = sem("alpha_ready")
        alpha_col = sem("alpha_col")
        w_ready = sem("w_ready")
        stats_done = sem("stats_done")
        finish_step = sem("finish_step")

        def at_least(eng, sem, value):
            if not isinstance(value, int) or value > 0:
                eng.wait_ge(sem, value)

        class Group:
            def __init__(self, i, slot):
                self.i, self.slot = i, slot
                self.n = i * RING + slot
                self.tail = isinstance(i, int) and self.n == GF
                self.sizes = [min(Q, TT - Q * s) for s in range(TQ)] if self.tail else [Q] * QG
                self.tiles = sum(self.sizes)
                self.first = isinstance(i, int) and self.n == 0

            def exists(self):
                return not isinstance(self.i, int) or self.n <= GF

            def after(self, k):
                s = self.slot + k
                return Group(self.i + s // RING, s % RING)

        TAIL = Group(GF // RING, GF % RING)

        def over_groups(eng, body):
            for n in range(RING):
                body(Group(0, n))
            with eng.Fori(1, LOOPS) as i:
                for slot in range(RING):
                    body(Group(i, slot))
            for n in range(LOOPS * RING, GF + 1):
                body(Group(n // RING, n % RING))

        def chunks(g):
            return -(-g.tiles // XL)

        def load_x(sp, g, c):
            k = c * XL
            ragged = g.tail and c == chunks(g) - 1
            m = min(XL, g.tiles - k) - ragged
            sp.dma_start(x_ring[:, g.slot, k:k + m, :],
                         x[bass.ds(g.n * (K * P) + k * P, m * P), :].rearrange("(k p) d -> p k d", p=P)
                         ).then_inc(x_in[g.slot][c], 16)
            if ragged:
                sp.wait_ge(x_zero, 1)
                sp.dma_start(x_ring[0:LAST, g.slot, k + m, :], x[N - LAST:N, :]).then_inc(x_in[g.slot][c], 16)

        def gather(pool, g, s):
            if s == 0:
                nc.gpsimd.tensor_copy(index_ring[:, g.slot, 0:g.tiles],
                                      src_cols[:, :, :].rearrange("p b q -> p (b q)")[:, bass.ds(g.n * K, g.tiles)]
                                      ).then_inc(index_ready, 1)
                pool.wait_ge(index_ready, g.n + 1)
                pool.nop(nofuse=True)
            for k in range(s * Q, s * Q + g.sizes[s]):
                pool.indirect_dma_start(
                    out=src_rows[:, g.slot, k, :], out_offset=None, in_=x[:, :],
                    in_offset=bass.IndirectOffsetOnAxis(ap=index_ring[:, g.slot, k:k + 1], axis=0)
                ).then_inc(src_in[g.slot][s], 16)

        pivots_in = sem("pivots_in")
        tables_out = sem("tables_out")
        iotas = sem("iotas")
        consts = sem("consts")
        dve = sem("dve")
        pivots_bc = sem("pivots_bc")
        run_ready = sem("run_ready")
        runs_in = sem("runs_in")
        start_ready = sem("start_ready")
        win_src_in = sem("win_src_in")
        win_dst_in = sem("win_dst_in")
        src_f_ready = sem("src_f_ready")
        rel_ready = sem("rel_ready")
        cols_ps = sem("cols_ps")
        cols_sb = sem("cols_sb")
        tally_ready = sem("tally_ready")
        verdict_ready = sem("verdict_ready")
        tally_ps = sem("tally_ps")

        edge_v = edge[0:EP * P, :].rearrange("(p t) d -> p t d", t=EP)

        def prologue_sync(sp):
            sp.dma_start(pivots_i[:, :], dst.rearrange("(a b) -> b a", b=RUN)[0:1, :],
                         allow_slow_non_contiguous=True).then_inc(pivots_in, 16)
            for to, a in ((wn[:, :], Wn), (we2[:, 0, :], We), (we2[:, 1, :], We)):
                sp.dma_start(to, a[:, :]).then_inc(weights_in, 16)
            sp.dma_start(wa[:, :], Wa.rearrange("a (k d) -> d (a k)", k=3),
                         allow_slow_non_contiguous=True).then_inc(weights_in, 16)

            def load_edge(c):
                if c >= 2:
                    sp.wait_ge(edge_v_used, c - 1)
                sp.dma_start(edge_v_in[:, c % 2, :, :],
                             edge_v[:, c * CH:(c + 1) * CH, :]).then_inc(edge_v_arrived[c % 2], 16)

            load_edge(0)
            for table, a in ((windows_src, src), (windows_dst, dst)):
                sp.dma_start(table[0:WR16, :], overlapped(a, WR16)).then_inc(tables_out, 16)
                sp.dma_start(table[WR16:WR, :], overlapped(a, WR - WR16, WR16)).then_inc(tables_out, 16)
            sp.wait_ge(runs_in, 16 * NB)
            load_edge(1)
            sp.dma_start(edge_rest[0:ER, :], edge[EP * P:E, :]).then_inc(edge_rest_in, 16)
            for c in range(2, VC):
                load_edge(c)
            for k in range(K // XL):
                load_x(sp, Group(0, 0), k)
            sp.wait_ge(score_ready, 2)
            sp.dma_start(edge_score[0:EP * P].rearrange("(p t) -> p t", t=EP), score[:, :]).then_inc(score_out, 16)
            sp.dma_start(edge_score[EP * P:E].rearrange("(p t) -> p t", t=1), score_rest[0:ER, :]).then_inc(score_out, 16)
            sp.wait_ge(score_out, 32)
            sp.dma_start(windows_edge[0:WR16, :], overlapped(edge_score, WR16)).then_inc(table_out, 16)
            sp.dma_start(windows_edge[WR16:WR, :], overlapped(edge_score, WR - WR16, WR16)).then_inc(table_out, 16)
            sp.wait_ge(tables_out, 64)

        def prologue_gpsimd(pool):
            nc.gpsimd.iota(first_i[:, :], pattern=[[P * P, NB]], base=0, channel_multiplier=P).then_inc(iotas, 1)
            nc.gpsimd.iota(node_iota_i[:, :], pattern=[[1, P]], base=0, channel_multiplier=0).then_inc(iotas, 1)
            nc.gpsimd.memset(ident[:, :], 0.0).then_inc(iotas, 1)
            pool.wait_ge(iotas, 3)
            nc.gpsimd.affine_select(out=ident[:, :], in_=ident[:, :], compare_op=ALU.not_equal, fill=1.0,
                                    base=0, pattern=[[-1, P]], channel_multiplier=1).then_inc(iotas, 1)
            pool.wait_ge(run_ready, 1)
            for b in range(NB):
                pool.indirect_dma_start(
                    out=runs[:, b, :], out_offset=None, in_=dst.rearrange("(a b) -> a b", b=RUN),
                    in_offset=bass.IndirectOffsetOnAxis(ap=run_i[:, b:b + 1], axis=0)).then_inc(runs_in, 16)
            pool.wait_ge(start_ready, 1)
            pool.wait_ge(tables_out, 64)
            for table, win, arrived in ((windows_src, win_src, win_src_in), (windows_dst, win_dst, win_dst_in)):
                for b in range(NB):
                    pool.indirect_dma_start(
                        out=win[:, b, :], out_offset=None, in_=table[:, :],
                        in_offset=bass.IndirectOffsetOnAxis(ap=start_k[:, b:b + 1], axis=0)).then_inc(arrived, 16)
            pool.wait_ge(cols_sb, NB)
            for s in range(QG):
                gather(pool, Group(0, 0), s)

        def prologue_tensor(pe):
            pe.wait_ge(consts, 1)
            nc.tensor.matmul(row_bank[:, 0:NR], ones[0:1, :], pivots[0:1, :], start=True, stop=True).then_inc(pivots_bc, 1)
            pe.wait_ge(iotas, 4)
            pe.wait_ge(weights_in, 64)
            nc.tensor.transpose(g_bank[0][:, 0:P], wn[:, :], ident[:, :])
            for bank, w, a, b in ((g_bank[1], D, wa[:, 0:1].to_broadcast([P, P]), wn[:, :]),
                                  (y_bank[0], P, wn[:, :], wa[:, 1:2].to_broadcast([P, P])),
                                  (y_bank[1], DE, wa[:, 2:3].to_broadcast([P, P]), we2[:, 0, :]),
                                  (xt_bank, D, wa[:, 1:2].to_broadcast([P, P]), wn[:, :]),
                                  (b_bank[0], 1, we2[:, :, :].rearrange("p r d -> p (r d)"), wa[:, 2:3])):
                last = nc.tensor.matmul(bank[:, 0:w], a, b, start=True, stop=True)
            last.then_inc(weights_ps, 1)
            pe.wait_ge(weights_sb, 1)

            def edge_chunk(c):
                pe.wait_ge(edge_t_arrived[c % 2], 16 * (c // 2 + 1))
                for b in range(PAIR_BANKS):
                    n = c * PAIR_BANKS + b
                    pairs = min(Q, CH // 2 - b * Q)
                    if n >= 2:
                        pe.wait_ge(pairs_sb, n - 1)
                    for k in range(pairs):
                        u = b * Q + k
                        last = nc.tensor.transpose(
                            (xt_bank, b_bank[0])[n % 2][:, k * P:(k + 1) * P],
                            edge_t_in[:, c % 2, 2 * u:2 * u + 2, :].rearrange("p t d -> p (t d)"), ident[:, :])
                    last.then_inc(pairs_ps, 1)
                    if n >= 1:
                        edge_dots(n - 1)

            def edge_dots(n):
                c, b = divmod(n, PAIR_BANKS)
                pe.wait_ge(pairs_sb, n + 1)
                for k in range(min(Q, CH // 2 - b * Q)):
                    at = c * CH + 2 * (b * Q + k)
                    last = nc.tensor.matmul(b_bank[1][:, at:at + 2], x_t[:, n % 2, k * P:(k + 1) * P],
                                            v_edge2[:, :], start=True, stop=True)
                last.then_inc(score_ps, 1)

            def window_cols(ready, rows, first_n):
                pe.wait_ge(ready, 1)
                for b in range(NB):
                    n = first_n + b
                    if n >= 4:
                        pe.wait_ge(cols_sb, n - 3)
                    bank = (g_bank + y_bank)[n % 4]
                    nc.tensor.transpose(bank[:, 0:P], rows[:, b, :], ident[:, :]).then_inc(cols_ps, 1)

            for c in range(TC):
                if c == SRC_COLS_AT:
                    window_cols(src_f_ready, src_f, 0)
                if c == REL_COLS_AT:
                    window_cols(rel_ready, rel, NB)
                edge_chunk(c)
            edge_dots(TC * PAIR_BANKS - 1)
            pe.wait_ge(tally_ready, 1)
            nc.tensor.matmul(row_bank[0:1, 0:2], ones[:, 0:1], tally[:, :], start=True, stop=True).then_inc(tally_ps, 1)

        def prologue_scalar(act):
            def load_edge(c):
                act.dma_start(edge_t_in[:, c % 2, :, :], edge_v[:, (VC + c) * CH:(VC + c + 1) * CH, :]
                              ).then_inc(edge_t_arrived[c % 2], 16)

            load_edge(0)
            act.wait_ge(weights_ps, 1)
            act.wait_ge(v_edge2_zero, 1)
            for to, bank, w in ((wn_t, g_bank[0], P), (v_src, g_bank[1], D), (v_dst, y_bank[0], P),
                                (v_edge, y_bank[1], DE), (v_dst_row, xt_bank, D)):
                nc.scalar.activation(to[:, :], bank[:, 0:w], ACT.Copy)
            for r in range(2):
                last = nc.scalar.activation(v_edge2[r * DE:(r + 1) * DE, r:r + 1],
                                            b_bank[0][r * DE:(r + 1) * DE, 0:1], ACT.Copy)
            last.then_inc(weights_sb, 1)

            def pairs_leave(c):
                for b in range(PAIR_BANKS):
                    n = c * PAIR_BANKS + b
                    w = min(Q, CH // 2 - b * Q) * P
                    act.wait_ge(pairs_ps, n + 1)
                    if n >= 2:
                        act.wait_ge(score_ps, n - 1)
                    nc.scalar.activation(x_t[:, n % 2, 0:w], (xt_bank, b_bank[0])[n % 2][:, 0:w],
                                         ACT.Copy).then_inc(pairs_sb, 1)
                if c + 2 < TC:
                    load_edge(c + 2)

            def window_cols_leave(first_n):
                for n in range(first_n, first_n + NB):
                    act.wait_ge(cols_ps, n + 1)
                    bank = (g_bank + y_bank)[n % 4]
                    to = src_cols[:, n, :] if n < NB else rel_cols[:, (n - NB) * P:(n - NB + 1) * P]
                    nc.scalar.activation(to, bank[:, 0:P], ACT.Copy).then_inc(cols_sb, 1)

            act.wait_ge(runs_in, 16 * NB)
            load_edge(1)
            for c in range(TC):
                if c == SRC_COLS_AT:
                    window_cols_leave(0)
                if c == REL_COLS_AT:
                    window_cols_leave(NB)
                pairs_leave(c)
            act.wait_ge(score_ps, TC * PAIR_BANKS)
            nc.scalar.activation(score[:, VC * CH:EP], b_bank[1][:, 0:TC * CH], ACT.Copy).then_inc(score_ready, 1)

        def prologue_vector(v):
            steps = [0]

            def chain(ins):
                steps[0] += 1
                ins.then_inc(dve, 1)
                v.wait_ge(dve, steps[0])

            def edge_chunk(c):
                now = edge_v_in[:, c % 2, :, :]
                v.wait_ge(edge_v_arrived[c % 2], 16 * (c // 2 + 1))
                chain(nc.vector.tensor_tensor(
                    now, now, v_edge[:, :].rearrange("p (t d) -> p t d", t=1).to_broadcast([P, CH, DE]), ALU.mult))
                nc.vector.tensor_reduce(score[:, c * CH:(c + 1) * CH], now, axis=AX.X, op=ALU.add).then_inc(edge_v_used, 1)

            nc.vector.memset(v_edge2[:, :], 0.0).then_inc(v_edge2_zero, 1)
            nc.vector.memset(ones[:, :], 1.0)
            v.wait_ge(pivots_in, 16)
            nc.vector.tensor_copy(pivots[:, :], pivots_i[:, :]).then_inc(consts, 1)
            v.wait_ge(iotas, 2)
            nc.vector.tensor_copy(node_iota[:, :], node_iota_i[:, :])
            chain(nc.vector.tensor_copy(first[:, :], first_i[:, :]))
            v.wait_ge(pivots_bc, 1)
            chain(nc.vector.tensor_tensor(
                below[:, :, 0:NR], row_bank[:, 0:NR].rearrange("p (b n) -> p b n", b=1).to_broadcast([P, NB, NR]),
                first[:, :].rearrange("p (b n) -> p b n", n=1).to_broadcast([P, NB, NR]), ALU.is_lt))
            chain(nc.vector.tensor_reduce(count[:, :], below[:, :, 0:NR], axis=AX.X, op=ALU.add))
            chain(nc.vector.tensor_scalar(run_f[:, :], count[:, :], -1.0, 0.0, ALU.add, ALU.max))
            nc.vector.tensor_copy(run_i[:, :], run_f[:, :]).then_inc(run_ready, 1)
            v.wait_ge(weights_sb, 1)
            edge_chunk(0)
            v.wait_ge(runs_in, 16 * NB)
            chain(nc.vector.tensor_tensor(
                below[:, :, 0:RUN], runs[:, :, :],
                first[:, :].rearrange("p (b n) -> p b n", n=1).to_broadcast([P, NB, RUN]), ALU.is_lt))
            chain(nc.vector.tensor_reduce(count[:, :], below[:, :, 0:RUN], axis=AX.X, op=ALU.add))
            chain(nc.vector.scalar_tensor_tensor(out=start_f[:, :], in0=run_f[:, :], scalar=float(RUN),
                                                 in1=count[:, :], op0=ALU.mult, op1=ALU.add))
            chain(nc.vector.tensor_copy(start_i[:, :], start_f[:, :]))
            shift_bits = STEP.bit_length() - 1
            chain(nc.vector.tensor_single_scalar(start_r[:, :], start_i[:, :], shift_bits, op=ALU.arith_shift_right))
            nc.vector.tensor_single_scalar(start_k[:, :], start_r[:, :], float(WR - 1), op=ALU.min).then_inc(start_ready, 1)
            for c in (1, 2):
                edge_chunk(c)
            v.wait_ge(win_src_in, 16 * NB)
            nc.vector.tensor_copy(src_f[:, :, :], win_src[:, :, :]).then_inc(src_f_ready, 1)
            edge_chunk(3)
            v.wait_ge(win_dst_in, 16 * NB)
            nc.vector.tensor_tensor(
                rel[:, :, :], win_dst[:, :, :],
                first[:, :].rearrange("p (b n) -> p b n", n=1).to_broadcast([P, NB, P]), ALU.subtract).then_inc(rel_ready, 1)
            v.wait_ge(rel_ready, 1)
            nc.vector.memset(same[:, :, 0:P + 2], 0.0)
            chain(nc.vector.tensor_single_scalar(in_tile[:, :, :], rel[:, :, :], 0.0, op=ALU.is_ge))
            chain(nc.vector.tensor_tensor(same[:, :, 1:P], rel[:, :, 1:P], rel[:, :, 0:P - 1], ALU.is_equal))
            chain(nc.vector.tensor_tensor(desc[:, :, 1:P], rel[:, :, 1:P], rel[:, :, 0:P - 1], ALU.is_lt))
            chain(nc.vector.scalar_tensor_tensor(out=hit[:, :, :], in0=rel[:, :, :], scalar=float(P),
                                                 in1=in_tile[:, :, :], op0=ALU.is_lt, op1=ALU.mult))
            nc.vector.tensor_reduce(tally[:, 0:1], hit[:, :, :], axis=AX.XY, op=ALU.add)
            nc.vector.tensor_reduce(tally[:, 1:2], desc[:, :, 1:P], axis=AX.XY, op=ALU.add).then_inc(tally_ready, 1)
            for c in range(4, VC):
                edge_chunk(c)
            v.wait_ge(edge_rest_in, 16)
            nc.vector.tensor_tensor_reduce(out=junk_a[0:ER, 0, 0, 0:DE], in0=edge_rest[0:ER, :], in1=v_edge[0:ER, :],
                                           scale=1.0, scalar=0.0, op0=ALU.mult, op1=ALU.add,
                                           accum_out=score_rest[0:ER, :]).then_inc(score_ready, 1)
            v.wait_ge(edge_v_used, VC)
            v.wait_ge(score_ready, 2)
            v.wait_ge(cols_sb, 2 * NB)
            v.wait_ge(tally_ps, 1)
            chain(nc.vector.tensor_copy(verdict[:, :], row_bank[0:1, 0:2]))
            chain(nc.vector.tensor_single_scalar(verdict[:, 1:2], verdict[:, 1:2], 0.0, op=ALU.is_equal))
            nc.vector.scalar_tensor_tensor(out=regular[:, :], in0=verdict[:, 0:1], scalar=float(E),
                                           in1=verdict[:, 1:2], op0=ALU.is_equal, op1=ALU.mult).then_inc(verdict_ready, 1)

        def load_rows(sp, g):
            sp.dma_start(rows_ring[:, g.slot, :], tile_rows[bass.ds(g.n * K, K), :]).then_inc(rows_in[g.slot], 16)

        def chunk_count(g, c):
            return (g.i + 1) * 16 + (16 if g.tail and c == chunks(g) - 1 else 0)

        def fast_sync(sp):
            tile_v = tile_rows.rearrange("(b p) c -> p b c", p=P)
            sp.dma_start(tile_v[:, :, 0:P + 2], same[:, :, :]).then_inc(same_out, 16)
            sp.wait_ge(table_out, 32)
            for k in range(K // XL):
                load_x(sp, Group(0, 1), k)
            sp.wait_ge(win_edge_in, 16 * NB)
            sp.dma_start(tile_v[:, :, P + 2:2 * P + 2], win_edge[:, :, :]).then_inc(same_out, 16)
            sp.wait_ge(same_out, 32)
            for n in range(3):
                load_rows(sp, Group(0, n))
            def store(g, c):
                quads = QG * g.n + min(2 * c + 2, len(g.sizes))
                by_v = len([p for p in NORM_V if p < quads]) if isinstance(g.i, int) else 0
                sp.wait_ge(normed, quads - by_v)
                at_least(sp, normed_v, by_v)
                k = c * XL
                ragged = g.tail and c == chunks(g) - 1
                m = min(XL, g.tiles - k) - ragged
                sp.dma_start(out[bass.ds(g.n * (K * P) + k * P, m * P), :].rearrange("(k p) d -> p k d", p=P),
                             x_ring[:, g.slot, k:k + m, :]).then_inc(stored[g.slot][c], 16)
                if ragged:
                    sp.dma_start(out[N - LAST:N, :], x_ring[0:LAST, g.slot, k + m, :]).then_inc(stored[g.slot][c], 16)

            def body(g):
                last, ahead = g.after(-1), g.after(3)
                if ahead.exists():
                    at_least(sp, alpha_ready, g.n)
                    load_rows(sp, ahead)
                for c in range(K // XL):
                    if g.first:
                        sp.wait_ge(y_ps, 2 * c - 1) if c else sp.wait_ge(alpha_ready, 1)
                        load_x(sp, g.after(2), c)
                    else:
                        store(last, c)
                    if ahead.exists() and c < chunks(ahead):
                        if not g.first:
                            sp.wait_ge(stored[last.slot][c], chunk_count(last, c))
                        load_x(sp, ahead, c)

            over_groups(sp, body)
            for c in range(chunks(TAIL)):
                store(TAIL, c)
            for slot in range(RING):
                for c in range(K // XL):
                    tail = slot == TAIL.slot and c < chunks(TAIL)
                    sp.wait_ge(stored[slot][c], chunk_count(TAIL, c) if tail else 16 * len(range(slot, GF, RING)))

        def fast_gpsimd(pool):
            for n in (1, 2):
                for s in range(QG):
                    gather(pool, Group(0, n), s)
                    if n == 1 and s == 0:
                        pool.wait_ge(table_out, 32)
                        for b in range(NB):
                            pool.indirect_dma_start(
                                out=win_edge[:, b, :], out_offset=None, in_=windows_edge[:, :],
                                in_offset=bass.IndirectOffsetOnAxis(ap=start_k[:, b:b + 1], axis=0)).then_inc(win_edge_in, 16)

            def body(g):
                ahead = g.after(3)
                if ahead.exists():
                    at_least(pool, g_ps, QG * g.n)
                    for s in range(len(ahead.sizes)):
                        if ahead.tail and s == TQ // 2:
                            c = chunks(ahead) - 1
                            pool.wait_ge(stored[ahead.slot][c], chunk_count(g.after(-1), c))
                            nc.gpsimd.memset(x_ring[:, ahead.slot, ahead.tiles - 1, :], 0.0).then_inc(x_zero, 1)
                        gather(pool, ahead, s)

            over_groups(pool, body)

        LEAD = QG + 5

        def quad_at(g, p):
            ahead = g.after(p // QG)
            return (ahead, p % QG) if ahead.exists() and p % QG < len(ahead.sizes) else None

        def has_a(g, s):
            return quad_at(g, s + LEAD)

        def has_b(g, s):
            return quad_at(g, s + LEAD - 1)

        def back(g, s, k):
            groups = -((s - k) // QG)
            if isinstance(g.i, int) and g.n < groups:
                return None
            return g.after(-groups), s - k + QG * groups

        B_LAST = 2 * QG - LEAD
        ROWS_AT = [4 * B_LAST + k for k in (0, 3, 4, 5, 6, 7, 9, 10, 11, 12, 13)]
        RSTD_AT = [4 * 2 + k for k in range(FINISHSTEPS + 1)]
        EXP_AT, COLS_AT = B_LAST + 1, B_LAST + 3
        NORM_LAG = QG + 5
        NORM_V = ([QG * (GF - 1) + s - NORM_LAG for s in range(1, QG, 2)] + [QG * GF + s - NORM_LAG for s in range(1, TQ, 2)]
                  + [QG * (GF - 1) + q for q in range(QG // 2, QG)] + [QG * GF + q for q in range(TQ)])

        def normed_by_v(g, q):
            return isinstance(g.i, int) and QG * g.n + q in NORM_V


        def pe_transpose(pe, g, q):
            n = QG * g.n + q
            if q * Q % XL == 0:
                pe.wait_ge(x_in[g.slot][q * Q // XL], chunk_count(g, q * Q // XL))
            at_least(pe, xt_sb, n)
            for k in range(g.sizes[q]):
                last = nc.tensor.transpose(xt_bank[:, k * P:(k + 1) * P], x_ring[:, g.slot, q * Q + k, :], ident[:, :])
            last.then_inc(xt_ps, 1)

        def pe_b(pe, g, q):
            n = QG * g.n + q
            w = g.sizes[q] * P
            at_least(pe, xt_sb, n + 1)
            at_least(pe, cols_done, n - 1)
            nc.tensor.matmul(b_bank[q % 2][:, 0:w], v_dst[:, :], x_t[:, q % 2, 0:w], start=True, stop=True).then_inc(b_ready, 1)

        def act_xt(act, g, q):
            n = QG * g.n + q
            w = g.sizes[q] * P
            act.wait_ge(xt_ps, n + 1)
            at_least(act, b_ready, n - 1)
            nc.scalar.activation(x_t[:, q % 2, 0:w], xt_bank[:, 0:w], ACT.Copy).then_inc(xt_sb, 1)

        def dve_a(v, g, q):
            if q == 0:
                nc.vector.tensor_copy(rel_ring[:, g.slot, 0:g.tiles],
                                      rel_cols[:, bass.ds(g.n * K, g.tiles)]).then_inc(rel_copied, 1)
            v.wait_ge(src_in[g.slot][q], (g.i + 1) * 64 if not g.tail else g.i * 64 + 16 * g.sizes[q])
            for k in range(q * Q, q * Q + g.sizes[q]):
                nc.vector.tensor_tensor_reduce(out=junk_a[:, q % 4, k % Q, :], in0=src_rows[:, g.slot, k, :], in1=v_src[:, :],
                                               scale=1.0, scalar=0.0, op0=ALU.mult, op1=ALU.add,
                                               accum_out=a_cols[:, g.slot, k:k + 1])
            if q == 0:
                v.wait_ge(rel_copied, g.n + 1)

        def matches_before(g, q):
            return QG // 2 * g.n + q // 2

        def dve_match(v, g, q):
            w = g.sizes[q]
            nc.vector.tensor_tensor(
                match[:, g.slot, q // 2, 0:w * P].rearrange("p (k n) -> p k n", n=P),
                node_iota[:, :].rearrange("p (k n) -> p k n", k=1).to_broadcast([P, w, P]),
                rel_ring[:, g.slot, q * Q:q * Q + w].rearrange("p (k n) -> p k n", n=1).to_broadcast([P, w, P]),
                ALU.is_equal).then_inc(match_ready, 1)

        def dve_b(v, g, q):
            v.wait_ge(b_ready, QG * g.n + q + 1)
            if q % 2:
                v.wait_ge(match_ready, matches_before(g, q) + 1)
            for k in range(q * Q, q * Q + g.sizes[q]):
                j = k - q * Q
                if q % 2:
                    last = nc.vector.tensor_tensor_reduce(
                        out=junk_b[:, q % 4, k % Q, :], in0=match[:, g.slot, q // 2, j * P:(j + 1) * P],
                        in1=b_bank[q % 2][:, j * P:(j + 1) * P], scale=1.0, scalar=0.0, op0=ALU.mult, op1=ALU.add,
                        accum_out=b_cols[:, g.slot, k:k + 1])
                    continue
                last = nc.vector.scalar_tensor_tensor(
                    out=junk_b[:, q % 4, k % Q, :], in0=node_iota[:, :], scalar=rel_ring[:, g.slot, k:k + 1],
                    in1=b_bank[q % 2][:, j * P:(j + 1) * P], op0=ALU.is_equal, op1=ALU.mult,
                    accum_out=b_cols[:, g.slot, k:k + 1])
            last.then_inc(cols_done, 1)

        def dve_rows(v, g, part):
            t = g.tiles
            base = ROWSTEPS * g.n
            kept = rows_ring[0:t, g.slot, 0:P + 1]
            if part == 0:
                v.wait_ge(cols_done, QG * g.n + len(g.sizes))
                nc.vector.tensor_tensor(ab_cols[:, g.slot, 0:t], a_cols[:, g.slot, 0:t], b_cols[:, g.slot, 0:t],
                                        ALU.add).then_inc(ab_ready, 1)
            if part == 1:
                v.wait_ge(rows_in[g.slot], (g.i + 1) * 16)
                nc.vector.tensor_scalar(pen[0:t, :], kept, -1.0, BIG, ALU.add, ALU.mult)
                v.wait_ge(ab_row, g.n + 1)
                nc.vector.tensor_tensor(zt[0:t, :], row_bank[0:t, 0:P], rows_ring[0:t, g.slot, P + 2:2 * P + 2],
                                        ALU.add).then_inc(rowstep, 1)
            if part == 2:
                v.wait_ge(rowstep, base + 1)
                nc.vector.scalar_tensor_tensor(out=z[0:t, :], in0=zt[0:t, :], scalar=SLOPE, in1=zt[0:t, :],
                                               op0=ALU.mult, op1=ALU.max).then_inc(rowstep, 1)
            if part == 3:
                v.wait_ge(rowstep, base + 2)
                nc.vector.tensor_tensor_scan(m_run[0:t, :], pen[0:t, 0:P], z[0:t, :], 0.0,
                                             ALU.add, ALU.max).then_inc(rowstep, 1)
            if part == 4:
                v.wait_ge(rowstep, base + 3)
                nc.vector.tensor_tensor_scan(m_seg[0:t, ::-1], pen[0:t, P:0:-1], m_run[0:t, ::-1], 0.0,
                                             ALU.add, ALU.max).then_inc(rowstep, 1)
            if part == 5:
                v.wait_ge(rowstep, base + 4)
                nc.vector.tensor_tensor(z_sub[0:t, :], z[0:t, :], m_seg[0:t, :], ALU.subtract).then_inc(sub_ready, 1)
            if part == 6:
                v.wait_ge(ex_ready, g.n + 1)
                nc.vector.tensor_tensor_scan(s_run[0:t, :], rows_ring[0:t, g.slot, 0:P], ex[0:t, :], 0.0,
                                             ALU.mult, ALU.add).then_inc(rowstep, 1)
            if part == 7:
                v.wait_ge(rowstep, base + 5)
                nc.vector.tensor_tensor_scan(s_seg[0:t, ::-1], rows_ring[0:t, g.slot, P:0:-1], s_run[0:t, ::-1], 0.0,
                                             ALU.mult, ALU.max).then_inc(rowstep, 1)
            if part == 8:
                v.wait_ge(rowstep, base + 6)
                nc.vector.scalar_tensor_tensor(out=s_run[0:t, :], in0=s_seg[0:t, :], scalar=0.0, in1=s_seg[0:t, :],
                                               op0=ALU.is_equal, op1=ALU.add).then_inc(rowstep, 1)
            if part == 9:
                v.wait_ge(rowstep, base + 7)
                nc.vector.reciprocal(s_inv[0:t, :], s_run[0:t, :]).then_inc(rowstep, 1)
            if part == 10:
                v.wait_ge(rowstep, base + 8)
                nc.vector.tensor_tensor(alpha[0:t, :], ex[0:t, :], s_inv[0:t, :], ALU.mult).then_inc(alpha_ready, 1)

        def pe_ab_rows(pe, g):
            pe.wait_ge(ab_ready, g.n + 1)
            nc.tensor.transpose(row_bank[0:g.tiles, 0:P], ab_cols[:, g.slot, 0:g.tiles], ident[:, :]).then_inc(ab_row, 1)

        def act_exp(act, g):
            act.wait_ge(sub_ready, g.n + 1)
            nc.scalar.activation(ex[0:g.tiles, :], z_sub[0:g.tiles, :], ACT.Exp).then_inc(ex_ready, 1)

        def pe_alpha_cols(pe, g):
            at_least(pe, alpha_ready, g.n + 1)
            pe.nop(nofuse=True)
            t = g.tiles
            nc.tensor.transpose(row_bank[:, 256:256 + t], alpha[0:t, :], ident[0:t, 0:t]).then_inc(alpha_col, 1)

        def act_w(act, g):
            act.wait_ge(alpha_col, g.n + 1)
            nc.scalar.activation(w_cols[:, g.slot, 0:g.tiles], row_bank[:, 256:256 + g.tiles], ACT.Copy).then_inc(w_ready, 1)

        def dve_select(v, g, s):
            n = QG * g.n + s
            at_least(v, g_ps, n - 1)
            for k in range(g.sizes[s]):
                col = s * Q + k
                last = nc.vector.tensor_scalar(
                    select[:, s % 2, k * P:(k + 1) * P], node_iota[:, :], rel_ring[:, g.slot, col:col + 1],
                    w_cols[:, g.slot, col:col + 1], ALU.is_equal, ALU.mult)
            last.then_inc(sel_even, 1)

        def act_select(act, g, s):
            n = QG * g.n + s
            if s == 1:
                act.wait_ge(w_ready, g.n + 1)
            act.wait_ge(match_ready, matches_before(g, s) + 1)
            at_least(act, g_ps, n - 1)
            for k in range(g.sizes[s]):
                col = s * Q + k
                last = nc.scalar.activation(select[:, 1, k * P:(k + 1) * P], match[:, g.slot, s // 2, k * P:(k + 1) * P],
                                            ACT.Copy, scale=w_cols[:, g.slot, col:col + 1])
            last.then_inc(sel_odd, 1)

        def pe_gather(pe, g, s):
            n = QG * g.n + s
            pe.wait_ge(sel_odd if s % 2 else sel_even, matches_before(g, s) + 1)
            at_least(pe, g_sb, n - 1)
            for k in range(g.sizes[s]):
                last = nc.tensor.matmul(g_bank[s % 2][:, k * P:(k + 1) * P], src_rows[:, g.slot, s * Q + k, :],
                                        select[:, s % 2, k * P:(k + 1) * P], start=True, stop=True)
            last.then_inc(g_ps, 1)

        def act_gather(act, g, s):
            n = QG * g.n + s
            w = g.sizes[s] * P
            at_least(act, g_ps, n + 1)
            at_least(act, y_ps, n - 1)
            nc.scalar.activation(gather_t[:, s % 2, 0:w], g_bank[s % 2][:, 0:w], ACT.Copy).then_inc(g_sb, 1)

        def pe_residual(pe, g, s):
            t = g.sizes[s]
            n = QG * g.n + s
            at_least(pe, y_sb, n - 1)
            nc.tensor.matmul(y_bank[s % 2][:, 0:t * D], ident[:, :],
                             x_ring[:, g.slot, s * Q:s * Q + t, :].rearrange("p k d -> p (k d)"), start=True, stop=False)

        def pe_project(pe, g, s):
            n = QG * g.n + s
            at_least(pe, g_sb, n + 1)
            t = g.sizes[s]
            for k in range(t):
                last = nc.tensor.matmul(y_bank[s % 2][:, k * D:(k + 1) * D], gather_t[:, s % 2, k * P:(k + 1) * P],
                                        wn_t[:, :], start=False, stop=(k == t - 1))
            last.then_inc(y_ps, 1)

        def dve_stats(v, g, s):
            v.wait_ge(y_sb, QG * g.n + s + 1)
            for k in range(g.sizes[s]):
                last = nc.vector.bn_stats(bn6[:, g.slot, s * Q + k, :], x_ring[:, g.slot, s * Q + k, :])
            last.then_inc(stats_done, 1)

        def act_y(act, g, s):
            t = g.sizes[s]
            act.wait_ge(y_ps, QG * g.n + s + 1)
            nc.scalar.activation(x_ring[:, g.slot, s * Q:s * Q + t, :].rearrange("p k d -> p (k d)"),
                                 y_bank[s % 2][:, 0:t * D], ACT.Copy).then_inc(y_sb, 1)

        def dve_rstd(v, g, part):
            t = g.tiles
            base = FINISHSTEPS * g.n
            even_mean, even_m2, odd_mean, odd_m2 = (bn6[:, g.slot, 0:t, c] for c in (1, 2, 4, 5))
            if part == 0:
                v.wait_ge(stats_done, QG * g.n + len(g.sizes))
                nc.vector.tensor_tensor(mean2[:, 0:t], even_mean, odd_mean, ALU.add)
                nc.vector.tensor_tensor(mean_gap[:, 0:t], even_mean, odd_mean, ALU.subtract)
                nc.vector.tensor_tensor(moment[:, 0:t], even_m2, odd_m2, ALU.add).then_inc(finish_step, 1)
            if part == 1:
                v.wait_ge(finish_step, base + 1)
                nc.vector.scalar_tensor_tensor(out=gap_sq[:, 0:t], in0=mean_gap[:, 0:t], scalar=0.25,
                                               in1=mean_gap[:, 0:t], op0=ALU.mult, op1=ALU.mult)
                nc.vector.tensor_scalar(moment_eps[:, 0:t], moment[:, 0:t], 1.0 / D, EPS, ALU.mult, ALU.add)
                nc.vector.tensor_scalar(minus_mean[:, 0:t], mean2[:, 0:t], -0.5, None, ALU.mult).then_inc(finish_step, 1)
            if part == 2:
                v.wait_ge(finish_step, base + 2)
                nc.vector.tensor_tensor(var_eps[:, 0:t], gap_sq[:, 0:t], moment_eps[:, 0:t], ALU.add).then_inc(finish_step, 1)
            if part == 3:
                v.wait_ge(finish_step, base + 3)
                nc.vector.tensor_single_scalar(half_bits[:, 0:t], var_eps[:, 0:t].bitcast(i32), 1,
                                               op=ALU.arith_shift_right).then_inc(finish_step, 1)
            if part == 4:
                v.wait_ge(finish_step, base + 4)
                nc.vector.tensor_scalar(guess[:, 0, 0:t], half_bits[:, 0:t], -1.0, GUESS, ALU.mult,
                                        ALU.add).then_inc(finish_step, 1)
            if 5 <= part < FINISHSTEPS:
                r, now = divmod(part - 5, 3)
                old = guess[:, r, 0:t].bitcast(fp32) if r == 0 else root[:, r - 1, 0:t]
                new = rstd[:, g.slot, 0:t] if r == NEWTON - 1 else root[:, r, 0:t]
                v.wait_ge(finish_step, base + part)
                if now == 0:
                    nc.vector.tensor_tensor(square[:, r, 0:t], old, old, ALU.mult).then_inc(finish_step, 1)
                if now == 1:
                    nc.vector.scalar_tensor_tensor(out=error[:, r, 0:t], in0=square[:, r, 0:t], scalar=-0.5,
                                                   in1=var_eps[:, 0:t], op0=ALU.mult, op1=ALU.mult).then_inc(finish_step, 1)
                if now == 2:
                    nc.vector.scalar_tensor_tensor(out=new, in0=error[:, r, 0:t], scalar=1.5, in1=old,
                                                   op0=ALU.add, op1=ALU.mult).then_inc(finish_step, 1)
            if part == FINISHSTEPS:
                v.wait_ge(finish_step, base + FINISHSTEPS)
                nc.vector.tensor_tensor(shift[:, g.slot, 0:t], minus_mean[:, 0:t], rstd[:, g.slot, 0:t],
                                        ALU.mult).then_inc(rstd_ready, 1)

        def act_norm(act, g, s):
            if s == 0 or normed_by_v(g, s - 1):
                act.wait_ge(y_sb, QG * g.n + len(g.sizes))
                act.wait_ge(rstd_ready, g.n + 1)
            for k in range(s * Q, s * Q + g.sizes[s]):
                last = nc.scalar.activation(x_ring[:, g.slot, k, :], x_ring[:, g.slot, k, :], ACT.Identity,
                                            scale=rstd[:, g.slot, k:k + 1], bias=shift[:, g.slot, k:k + 1])
            last.then_inc(normed, 1)

        def dve_norm(v, g, s):
            v.wait_ge(rstd_ready, g.n + 1)
            for k in range(s * Q, s * Q + g.sizes[s]):
                last = nc.vector.tensor_scalar(x_ring[:, g.slot, k, :], x_ring[:, g.slot, k, :], rstd[:, g.slot, k:k + 1],
                                               shift[:, g.slot, k:k + 1], ALU.mult, ALU.add)
            last.then_inc(normed_v, 1)

        def fast_tensor(pe):
            for p in range(LEAD):
                pe_transpose(pe, *quad_at(Group(0, 0), p))
                if p:
                    pe_b(pe, *quad_at(Group(0, 0), p - 1))
                if p == QG + 1:
                    pe_ab_rows(pe, Group(0, 0))
            pe_alpha_cols(pe, Group(0, 0))

            def body(g):
                for s in range(len(g.sizes)):
                    if has_b(g, s):
                        pe_b(pe, *has_b(g, s))
                    if has_a(g, s):
                        pe_transpose(pe, *has_a(g, s))
                    pe_gather(pe, g, s)
                    if back(g, s, 1):
                        pe_residual(pe, *back(g, s, 1))
                        pe_project(pe, *back(g, s, 1))
                    if s == B_LAST and g.after(1).exists():
                        pe_ab_rows(pe, g.after(1))
                    if s == COLS_AT and g.after(1).exists():
                        pe_alpha_cols(pe, g.after(1))
                if g.tail:
                    pe_residual(pe, g, TQ - 1)
                    pe_project(pe, g, TQ - 1)

            over_groups(pe, body)

        def fast_scalar(act):
            for p in range(LEAD):
                act_xt(act, *quad_at(Group(0, 0), p))
            act_exp(act, Group(0, 0))
            act_w(act, Group(0, 0))
            act_select(act, Group(0, 0), 1)

            def body(g):
                for s in range(len(g.sizes)):
                    if has_a(g, s):
                        act_xt(act, *has_a(g, s))
                    act_gather(act, g, s)
                    if back(g, s, NORM_LAG) and not normed_by_v(*back(g, s, NORM_LAG)):
                        act_norm(act, *back(g, s, NORM_LAG))
                    if back(g, s, 1):
                        act_y(act, *back(g, s, 1))
                    if s % 2 and quad_at(g, s + 2):
                        act_select(act, *quad_at(g, s + 2))
                    if s == EXP_AT and g.after(1).exists():
                        act_exp(act, g.after(1))
                    if s == COLS_AT and g.after(1).exists():
                        act_w(act, g.after(1))
                if g.tail:
                    act_y(act, g, TQ - 1)
                    for p in range(QG * GF + TQ - NORM_LAG, QG * GF):
                        if not normed_by_v(*quad_at(Group(0, 0), p)):
                            act_norm(act, *quad_at(Group(0, 0), p))

            over_groups(act, body)

        def fast_vector(v):
            for p in range(LEAD):
                g, q = quad_at(Group(0, 0), p)
                dve_a(v, g, q)
                if q % 2:
                    dve_match(v, g, q)
                if p:
                    dve_b(v, *quad_at(Group(0, 0), p - 1))
                if p == QG:
                    dve_rows(v, Group(0, 0), 0)
                if p in (LEAD - 3, LEAD - 2):
                    for part in range(1, 6) if p == LEAD - 3 else range(6, len(ROWS_AT)):
                        dve_rows(v, Group(0, 0), part)
            v.wait_ge(w_ready, 1)
            dve_select(v, Group(0, 0), 0)

            def chains(g, at):
                if g.tail:
                    part = 2 * (at - RSTD_AT[0])
                    for now in (part, part + 1):
                        if 0 <= now < len(RSTD_AT):
                            dve_rstd(v, g.after(-1), now)
                    return
                if at in ROWS_AT and g.after(1).exists():
                    dve_rows(v, g.after(1), ROWS_AT.index(at))
                if at in RSTD_AT and not g.first:
                    dve_rstd(v, g.after(-1), RSTD_AT.index(at))

            def body(g):
                nxt = g.after(1)
                for s in range(len(g.sizes)):
                    if has_b(g, s):
                        dve_b(v, *has_b(g, s))
                    chains(g, 4 * s)
                    if s + 1 < len(g.sizes):
                        if s % 2:
                            dve_select(v, g, s + 1)
                    elif nxt.exists():
                        v.wait_ge(w_ready, nxt.n + 1)
                        dve_select(v, nxt, 0)
                    chains(g, 4 * s + 1)
                    if has_a(g, s):
                        dve_a(v, *has_a(g, s))
                        if has_a(g, s)[1] % 2:
                            dve_match(v, *has_a(g, s))
                    chains(g, 4 * s + 2)
                    if back(g, s, 2):
                        dve_stats(v, *back(g, s, 2))
                    if back(g, s, NORM_LAG) and normed_by_v(*back(g, s, NORM_LAG)):
                        dve_norm(v, *back(g, s, NORM_LAG))
                    chains(g, 4 * s + 3)
                if g.tail:
                    for at in range(4 * TQ, 4 * QG):
                        chains(g, at)
                    dve_stats(v, g, TQ - 2)
                    dve_stats(v, g, TQ - 1)
                    for part in range(len(RSTD_AT)):
                        dve_rstd(v, g, part)
                        if part % 4 == 0:
                            dve_norm(v, g.after(-1), QG // 2 + part // 4)
                    for s in range(TQ):
                        dve_norm(v, g, s)

            over_groups(v, body)

        ET = -(-E // P)
        EL = E - (ET - 1) * P
        SW = D + 2
        EDGE_STEPS, NODE_STEPS = 15, 6
        state = nc.dram_tensor("state", (N, SW), fp32, kind="Internal").ap()
        room = x_ring[:, 0:2, :, :].rearrange("p r k d -> p (r k d)")
        used = [0]

        def part(width, dt=fp32):
            at = used[0]
            used[0] += -(-width // 8) * 8
            return room[:, at:at + width] if dt == fp32 else room[:, at:at + width].bitcast(dt)

        src_col, dst_col = part(ET, i32), part(ET, i32)
        dst_col_f = part(ET)
        src_now, dst_now, scatter_to = part(1, i32), part(1, i32), part(1, i32)
        dst_now_f, first_before, scatter_f = part(1), part(1), part(1)
        blank = part(SW)
        lower = part(P)
        from_rows, to_rows, old, new = part(D), part(D), part(SW), part(SW)
        edge_now = part(DE)
        products, same_dst, before, penalty, z_pen = part(D), part(P), part(P), part(P), part(P)
        dots, z_pre, z_now, m_tile, m_new = part(3), part(1), part(1), part(1), part(1)
        deltas, exps = part(2), part(2)
        weighted = part(D + 1)
        x_now, y_now, y_out = part(D), part(D), part(D)
        s_one, s_rec, mean, stats, aggr, var_e, std, std_inv = (part(w) for w in (1, 1, D, 6, 2, 1, 1, 1))
        mean_t = part(P)

        g_set = sem("g_set")
        g_cols_in = sem("g_cols_in")
        g_blank = sem("g_blank")
        g_prep = sem("g_prep")
        g_edge_in = sem("g_edge_in")
        g_index = sem("g_index")
        g_rows_in = sem("g_rows_in")
        g_z = sem("g_z")
        g_bc = sem("g_bc")
        g_delta = sem("g_delta")
        g_exp = sem("g_exp")
        g_weighted = sem("g_weighted")
        g_sum = sem("g_sum")
        g_new = sem("g_new")
        g_scattered = sem("g_scattered")
        g_dve = sem("g_dve")
        g_state_in = sem("g_state_in")
        g_mean = sem("g_mean")
        g_mean_ps = sem("g_mean_ps")
        g_mean_t = sem("g_mean_t")
        g_h = sem("g_h")
        g_var = sem("g_var")
        g_std = sem("g_std")
        g_y = sem("g_y")
        g_stored = sem("g_stored")

        def over_edges(eng, body):
            with eng.Fori(0, ET - 1) as t:
                body(t, P)
            body(ET - 1, EL)

        def over_nodes(eng, body):
            with eng.Fori(0, NT - 1) as t:
                body(t, P)
            body(NT - 1, LAST)

        class Steps:
            def __init__(self, v, base, per_iteration):
                self.v, self.base, self.per, self.k = v, base, per_iteration, 0

            def __call__(self, ins):
                self.k += 1
                ins.then_inc(g_dve, 1)
                self.v.wait_ge(g_dve, self.base + self.k)

            def end(self):
                assert self.k == self.per, self.k

        def general_sync(sp):
            sp.wait_ge(table_out, 32)
            sp.wait_ge(g_set, 1)
            for col, a in ((src_col, src), (dst_col, dst)):
                sp.dma_start(col[:, 0:ET - 1], a[0:(ET - 1) * P].rearrange("(t p) -> p t", p=P),
                             allow_slow_non_contiguous=True).then_inc(g_cols_in, 16)
                sp.dma_start(col[0:EL, ET - 1:ET], a[(ET - 1) * P:E].rearrange("(p t) -> p t", t=1)).then_inc(g_cols_in, 16)

            def clear(t, rows):
                sp.dma_start(state[bass.ds(t * P, rows), :], blank[0:rows, :]).then_inc(g_blank, 16)
                sp.wait_ge(g_blank, 16 * (t + 1))
                sp.nop(nofuse=True)

            over_nodes(sp, clear)

            def edges(t, rows):
                sp.dma_start(edge_now[0:rows, :], edge[bass.ds(t * P, rows), :]).then_inc(g_edge_in, 16)
                sp.wait_ge(g_scattered, 16 * (t + 1))
                sp.nop(nofuse=True)

            over_edges(sp, edges)

            def nodes(t, rows):
                sp.dma_start(old[0:rows, :], state[bass.ds(t * P, rows), :]).then_inc(g_state_in, 16)
                sp.dma_start(x_now[0:rows, :], x[bass.ds(t * P, rows), :]).then_inc(g_state_in, 16)
                sp.wait_ge(g_y, t + 1)
                sp.dma_start(out[bass.ds(t * P, rows), :], y_out[0:rows, :]).then_inc(g_stored, 16)
                sp.wait_ge(g_stored, 16 * (t + 1))
                sp.nop(nofuse=True)

            over_nodes(sp, nodes)

        def general_gpsimd(pool):
            for k in range(K // XL):
                pool.wait_ge(x_in[0][k], 16)
            nc.gpsimd.memset(room[:, 0:used[0]], 0.0).then_inc(g_prep, 1)
            pool.wait_ge(g_prep, 1)
            nc.gpsimd.memset(dst_col_f[:, :], float(N))
            nc.gpsimd.memset(dst_col[:, :], N)
            nc.gpsimd.memset(blank[:, D + 1:SW], -BIG)
            nc.gpsimd.memset(lower[:, :], 1.0).then_inc(g_prep, 1)
            pool.wait_ge(g_prep, 2)
            nc.gpsimd.affine_select(out=lower[:, :], in_=lower[:, :], compare_op=ALU.is_ge, fill=0.0,
                                    base=-1, pattern=[[-1, P]], channel_multiplier=1).then_inc(g_set, 1)
            pool.wait_ge(g_cols_in, 64)
            pool.wait_ge(g_blank, 16 * NT)

            def edges(t, rows):
                nc.gpsimd.tensor_copy(src_now[:, :], src_col[:, bass.ds(t, 1)])
                nc.gpsimd.tensor_copy(dst_now[:, :], dst_col[:, bass.ds(t, 1)]).then_inc(g_index, 1)
                pool.wait_ge(g_index, t + 1)
                pool.nop(nofuse=True)
                for rows_sb, table, idx in ((from_rows, x, src_now), (to_rows, x, dst_now), (old, state, dst_now)):
                    pool.indirect_dma_start(
                        out=rows_sb[:, :], out_offset=None, in_=table[:, :],
                        in_offset=bass.IndirectOffsetOnAxis(ap=idx[:, 0:1], axis=0),
                        bounds_check=N - 1, oob_is_err=False).then_inc(g_rows_in, 16)
                pool.wait_ge(g_new, t + 1)
                pool.nop(nofuse=True)
                pool.indirect_dma_start(
                    out=state[:, :], out_offset=bass.IndirectOffsetOnAxis(ap=scatter_to[:, 0:1], axis=0),
                    in_=new[:, :], in_offset=None, bounds_check=N - 1, oob_is_err=False).then_inc(g_scattered, 16)
                pool.wait_ge(g_scattered, 16 * (t + 1))
                pool.nop(nofuse=True)

            over_edges(pool, edges)

        def general_tensor(pe):
            def edges(t, rows):
                pe.wait_ge(g_z, t + 1)
                nc.tensor.matmul(row_bank[:, 0:P], z_now[:, 0:1].to_broadcast([P, P]), ident[:, :], start=True, stop=True)
                nc.tensor.matmul(row_bank[:, P:2 * P], dst_now_f[:, 0:1].to_broadcast([P, P]), ident[:, :], start=True,
                                 stop=True).then_inc(g_bc, 1)
                pe.wait_ge(g_weighted, t + 1)
                nc.tensor.matmul(xt_bank[:, 0:D + 1], same_dst[:, :], weighted[:, :], start=True, stop=True).then_inc(g_sum, 1)

            over_edges(pe, edges)

            def nodes(t, rows):
                pe.wait_ge(g_mean, t + 1)
                nc.tensor.transpose(b_bank[0][:, 0:P], mean[:, :], ident[:, :]).then_inc(g_mean_ps, 1)
                pe.wait_ge(g_mean_t, t + 1)
                nc.tensor.matmul(b_bank[1][:, 0:D], mean_t[:, :], wn_t[:, :], start=True, stop=True).then_inc(g_h, 1)

            over_nodes(pe, nodes)

        def general_scalar(act):
            def edges(t, rows):
                act.wait_ge(g_delta, t + 1)
                nc.scalar.activation(exps[:, :], deltas[:, :], ACT.Exp).then_inc(g_exp, 1)

            over_edges(act, edges)

            def nodes(t, rows):
                act.wait_ge(g_mean_ps, t + 1)
                nc.scalar.activation(mean_t[:, :], b_bank[0][:, 0:P], ACT.Copy).then_inc(g_mean_t, 1)
                act.wait_ge(g_var, t + 1)
                nc.scalar.activation(std[:, :], var_e[:, :], ACT.Sqrt).then_inc(g_std, 1)

            over_nodes(act, nodes)

        def general_vector(v):
            v.wait_ge(g_cols_in, 64)
            nc.vector.tensor_copy(dst_col_f[:, :], dst_col[:, :]).then_inc(g_dve, 1)
            v.wait_ge(g_dve, 1)

            def edges(t, rows):
                step = Steps(v, 1 + EDGE_STEPS * t, EDGE_STEPS)
                nc.vector.tensor_copy(dst_now_f[:, :], dst_col_f[:, bass.ds(t, 1)])
                v.wait_ge(g_edge_in, 16 * (t + 1))
                v.wait_ge(g_rows_in, 48 * (t + 1))
                for n, (a, b, w) in enumerate(((from_rows, v_src, D), (to_rows, v_dst_row, D), (edge_now, v_edge, DE))):
                    step(nc.vector.tensor_tensor(products[:, 0:w], a[:, :], b[:, :], ALU.mult))
                    step(nc.vector.tensor_reduce(dots[:, n:n + 1], products[:, 0:w], axis=AX.X, op=ALU.add))
                step(nc.vector.tensor_reduce(z_pre[:, :], dots[:, :], axis=AX.X, op=ALU.add))
                nc.vector.scalar_tensor_tensor(out=z_now[:, :], in0=z_pre[:, :], scalar=SLOPE, in1=z_pre[:, :],
                                               op0=ALU.mult, op1=ALU.max).then_inc(g_z, 1)
                v.wait_ge(g_bc, t + 1)
                step(nc.vector.tensor_tensor(same_dst[:, :], row_bank[:, P:2 * P], dst_now_f[:, 0:1].to_broadcast([P, P]),
                                             ALU.is_equal))
                nc.vector.tensor_tensor(before[:, :], same_dst[:, :], lower[:, :], ALU.mult)
                step(nc.vector.tensor_scalar(penalty[:, :], same_dst[:, :], -1.0, BIG, ALU.add, ALU.mult))
                nc.vector.tensor_reduce(first_before[:, :], before[:, :], axis=AX.X, op=ALU.max)
                step(nc.vector.tensor_tensor(z_pen[:, :], row_bank[:, 0:P], penalty[:, :], ALU.add))
                step(nc.vector.tensor_reduce(m_tile[:, :], z_pen[:, :], axis=AX.X, op=ALU.max))
                nc.vector.scalar_tensor_tensor(out=scatter_to[:, :], in0=first_before[:, :], scalar=float(N),
                                               in1=dst_now_f[:, :], op0=ALU.mult, op1=ALU.add)
                step(nc.vector.tensor_tensor(m_new[:, :], m_tile[:, :], old[:, D + 1:SW], ALU.max))
                nc.vector.tensor_tensor(deltas[:, 0:1], z_now[:, :], m_new[:, :], ALU.subtract)
                nc.vector.tensor_copy(new[:, D + 1:SW], m_new[:, :])
                nc.vector.tensor_tensor(deltas[:, 1:2], old[:, D + 1:SW], m_new[:, :], ALU.subtract).then_inc(g_delta, 1)
                v.wait_ge(g_exp, t + 1)
                nc.vector.tensor_copy(weighted[:, D:D + 1], exps[:, 0:1])
                nc.vector.tensor_tensor(weighted[:, 0:D], from_rows[:, :], exps[:, 0:1].to_broadcast([P, D]),
                                        ALU.mult).then_inc(g_weighted, 1)
                step(nc.vector.tensor_tensor(old[:, 0:D + 1], old[:, 0:D + 1], exps[:, 1:2].to_broadcast([P, D + 1]), ALU.mult))
                v.wait_ge(g_sum, t + 1)
                step(nc.vector.tensor_tensor(new[:, 0:D + 1], xt_bank[:, 0:D + 1], old[:, 0:D + 1], ALU.add))
                step(nc.vector.tensor_copy(dots[:, 0:1], m_new[:, :]))
                nc.vector.tensor_copy(dots[:, 1:2], m_new[:, :]).then_inc(g_new, 1)
                v.wait_ge(g_scattered, 16 * (t + 1))
                step.end()

            over_edges(v, edges)

            def nodes(t, rows):
                step = Steps(v, 1 + EDGE_STEPS * ET + NODE_STEPS * t, NODE_STEPS)
                v.wait_ge(g_state_in, 32 * (t + 1))
                step(nc.vector.scalar_tensor_tensor(out=s_one[:, :], in0=old[:, D:D + 1], scalar=0.0, in1=old[:, D:D + 1],
                                                    op0=ALU.is_equal, op1=ALU.add))
                step(nc.vector.reciprocal(s_rec[:, :], s_one[:, :]))
                nc.vector.tensor_tensor(mean[:, :], old[:, 0:D], s_rec[:, 0:1].to_broadcast([P, D]), ALU.mult).then_inc(g_mean, 1)
                v.wait_ge(g_h, t + 1)
                step(nc.vector.tensor_tensor(y_now[:, :], b_bank[1][:, 0:D], x_now[:, :], ALU.add))
                step(nc.vector.bn_stats(stats[:, :], y_now[:, :]))
                v.nop(nofuse=True)
                step(nc.vector.bn_aggr(aggr[:, :], stats[:, :]))
                nc.vector.tensor_scalar(var_e[:, :], aggr[:, 1:2], EPS, None, ALU.add).then_inc(g_var, 1)
                v.wait_ge(g_std, t + 1)
                step(nc.vector.reciprocal(std_inv[:, :], std[:, :]))
                nc.vector.tensor_scalar(y_out[:, :], y_now[:, :], aggr[:, 0:1], std_inv[:, 0:1], ALU.subtract,
                                        ALU.mult).then_inc(g_y, 1)
                v.wait_ge(g_stored, 16 * (t + 1))
                step.end()

            over_nodes(v, nodes)

        with nc.Block() as block:
            @block.sync
            def _(sp):
                prologue_sync(sp)
                sp.wait_ge(verdict_ready, 1)
                sp.nop(nofuse=True)
                ok = sp.value_load(regular[0:1, 0:1], min_val=0, max_val=1)
                with sp.If(ok):
                    fast_sync(sp)
                with sp.Else():
                    general_sync(sp)

            @block.gpsimd
            def _(pool):
                prologue_gpsimd(pool)
                pool.wait_ge(verdict_ready, 1)
                pool.nop(nofuse=True)
                ok = pool.value_load(regular[0:1, 0:1], min_val=0, max_val=1)
                with pool.If(ok):
                    fast_gpsimd(pool)
                with pool.Else():
                    general_gpsimd(pool)

            @block.tensor
            def _(pe):
                prologue_tensor(pe)
                pe.wait_ge(verdict_ready, 1)
                pe.nop(nofuse=True)
                ok = pe.value_load(regular[0:1, 0:1], min_val=0, max_val=1)
                with pe.If(ok):
                    fast_tensor(pe)
                with pe.Else():
                    general_tensor(pe)

            @block.scalar
            def _(act):
                prologue_scalar(act)
                act.wait_ge(verdict_ready, 1)
                act.nop(nofuse=True)
                ok = act.value_load(regular[0:1, 0:1], min_val=0, max_val=1)
                with act.If(ok):
                    fast_scalar(act)
                with act.Else():
                    general_scalar(act)

            @block.vector
            def _(v):
                prologue_vector(v)
                v.wait_ge(verdict_ready, 1)
                v.nop(nofuse=True)
                ok = v.value_load(regular[0:1, 0:1], min_val=0, max_val=1)
                with v.If(ok):
                    fast_vector(v)
                with v.Else():
                    general_vector(v)


_INS = ["x", "src", "dst", "edge_attr_64", "L0_gnn_Wn", "L0_gnn_We", "L0_gnn_Wa"]


def kernel(**inputs):
    import numpy as _np
    import concourse.bacc as _bacc
    from concourse import mybir as _mybir
    from concourse.bass_utils import run_bass_kernel_spmd as _run

    nc = _bacc.Bacc("TRN2", target_bir_lowering=False, num_devices=1)
    arrays, args = {}, []
    for name in _INS:
        a = _np.ascontiguousarray(inputs[name])
        arrays[f"in_{name}"] = a
        args.append(nc.dram_tensor(f"in_{name}", a.shape, _mybir.dt.from_np(a.dtype), kind="ExternalInput").ap())
    out = nc.dram_tensor("out_0", tuple(inputs["x"].shape), _mybir.dt.float32, kind="ExternalOutput").ap()
    gnn_layer(nc, *args, out)
    r = _run(nc, [arrays], core_ids=[0])
    return r.results[0]["out_0"]
```
